# Optimizing a Trainium2 kernel written in Bass

```python
import numpy as np
import jax
import jax.numpy as jnp

def _softmax(x, axis=-1):
    return jax.nn.softmax(x, axis=axis)

def _gelu(x):
    return jax.nn.gelu(x, approximate=True)

def _silu(x):
    return jax.nn.silu(x)

def _sigmoid(x):
    return jax.nn.sigmoid(x)

def _layernorm(x, axis=-1, eps=1e-05):
    m = jnp.mean(x, axis=axis, keepdims=True)
    v = jnp.var(x, axis=axis, keepdims=True)
    return (x - m) / jnp.sqrt(v + eps)

def _scatter_add(tgt, idx, src, axis=0):
    return tgt.at[idx].add(src)

def _segment_sum(src, seg, n):
    return jax.ops.segment_sum(src, seg, n)
kernel_name = 'mk_gnn_resnorm_d1_gnn_r8_9dfea2'

def setup_inputs(seed: int=0):
    np.random.seed(seed)
    _w = jnp.asarray

    def _rec_inputs():
        import jax
        import jax.numpy as jnp
        _gk = jax.random.key(seed)
        x = -0.0004287 + 1 * jax.random.normal(jax.random.fold_in(_gk, 1), (12500, 160), jnp.float32)
        src = jax.random.randint(jax.random.fold_in(_gk, 2), (400000,), 0, 12500, jnp.int32)
        dst = jnp.minimum((12500 * jax.random.uniform(jax.random.fold_in(_gk, 3), (400000,)) ** 2.0).astype(jnp.int32), 99999)
        _o = jnp.argsort(dst, stable=True)
        src = src[_o]
        dst = dst[_o]
        edge_attr_10 = jax.random.uniform(jax.random.fold_in(_gk, 12), (400000, 10), jnp.float32, 0.0, 1)
        edge_attr_4 = 0.000486536 + 0.999406 * jax.random.normal(jax.random.fold_in(_gk, 13), (400000, 4), jnp.float32)
        node_vec1 = -0.00786984 + 0.999612 * jax.random.normal(jax.random.fold_in(_gk, 14), (12500, 1), jnp.float32)
        node_vec1_n2 = -0.00786984 + 0.999612 * jax.random.normal(jax.random.fold_in(_gk, 15), (12500, 1), jnp.float32)
        node_vec1_n3 = -0.00786984 + 0.999612 * jax.random.normal(jax.random.fold_in(_gk, 16), (12500, 1), jnp.float32)
        return (x, src, dst, edge_attr_10, edge_attr_4, node_vec1, node_vec1_n2, node_vec1_n3)
    x, src, dst, edge_attr_10, edge_attr_4, node_vec1, node_vec1_n2, node_vec1_n3 = _rec_inputs()

    def _L0_gnn_setup():
        import jax, jax.numpy as jnp
        import numpy as np
        N = 3125
        E = 50000
        S = 64
        V = 32
        NB = 10
        H = 100
        WN = 192
        MID = 96
        NUM_NEIGHBORS = 16.0
        C_S = float(np.sin(np.pi / 8.0))
        C_X = float(np.cos(np.pi / 8.0))
        SQRT3 = float(np.sqrt(3.0))

        def fctp_scalar_attr(xs, xv, attr, Ws, Wv):
            s = xs * attr @ Ws
            v = jnp.einsum('nuc,uo->noc', xv * attr[:, :, None], Wv)
            return (s, v)
        key = jax.random.key(seed)
        k = jax.random.split(key, 24)

        def w(i, shape):
            return jax.random.normal(k[i], shape, jnp.float32) / np.sqrt(float(shape[0]))
        return {'node_input': jax.random.normal(k[0], (N, S + 3 * V), jnp.float32), 'node_attr': jax.random.normal(k[1], (N, 1), jnp.float32), 'node_crystal_attr': jax.random.normal(k[2], (N, 1), jnp.float32), 'sym_mask': jax.random.normal(k[3], (N, 1), jnp.float32), 'edge_attr': jax.random.normal(k[4], (E, 4), jnp.float32), 'edge_length_embedded': jax.random.uniform(k[5], (E, NB), dtype=jnp.float32), 'edge_src': jax.random.randint(k[6], (E,), 0, N), 'edge_dst': jax.random.randint(k[7], (E,), 0, N), 'Ws_sc_a': w(8, (S, S)), 'Wv_sc_a': w(9, (V, V)), 'Ws_sc_c': w(10, (S, S)), 'Wv_sc_c': w(11, (V, V)), 'Ws_l1_a': w(12, (S, S)), 'Wv_l1_a': w(13, (V, V)), 'Ws_l1_c': w(14, (S, S)), 'Wv_l1_c': w(15, (V, V)), 'W_fc1': w(16, (NB, H)), 'W_fc2': w(17, (H, WN)), 'Ws_l2_a': w(18, (MID, MID)), 'Wv_l2_a': w(19, (MID, MID)), 'Ws_l2_c': w(20, (MID, MID)), 'Wv_l2_c': w(21, (MID, MID)), 'Ws_l3': w(22, (MID, S)), 'Wv_l3': w(23, (MID, V))}
    _L0_gnn_all = _L0_gnn_setup()
    _L0_gnn_in = {k: v for k, v in _L0_gnn_all.items() if k in ('Ws_sc_a', 'Wv_sc_a', 'Ws_sc_c', 'Wv_sc_c', 'Ws_l1_a', 'Wv_l1_a', 'Ws_l1_c', 'Wv_l1_c', 'W_fc1', 'W_fc2', 'Ws_l2_a', 'Wv_l2_a', 'Ws_l2_c', 'Wv_l2_c', 'Ws_l3', 'Wv_l3')}
    del _L0_gnn_all
    return {'x': x, 'src': src, 'dst': dst, 'edge_attr_10': edge_attr_10, 'edge_attr_4': edge_attr_4, 'node_vec1': node_vec1, 'node_vec1_n2': node_vec1_n2, 'node_vec1_n3': node_vec1_n3, 'L0_gnn_Ws_sc_a': _L0_gnn_in['Ws_sc_a'], 'L0_gnn_Wv_sc_a': _L0_gnn_in['Wv_sc_a'], 'L0_gnn_Ws_sc_c': _L0_gnn_in['Ws_sc_c'], 'L0_gnn_Wv_sc_c': _L0_gnn_in['Wv_sc_c'], 'L0_gnn_Ws_l1_a': _L0_gnn_in['Ws_l1_a'], 'L0_gnn_Wv_l1_a': _L0_gnn_in['Wv_l1_a'], 'L0_gnn_Ws_l1_c': _L0_gnn_in['Ws_l1_c'], 'L0_gnn_Wv_l1_c': _L0_gnn_in['Wv_l1_c'], 'L0_gnn_W_fc1': _L0_gnn_in['W_fc1'], 'L0_gnn_W_fc2': _L0_gnn_in['W_fc2'], 'L0_gnn_Ws_l2_a': _L0_gnn_in['Ws_l2_a'], 'L0_gnn_Wv_l2_a': _L0_gnn_in['Wv_l2_a'], 'L0_gnn_Ws_l2_c': _L0_gnn_in['Ws_l2_c'], 'L0_gnn_Wv_l2_c': _L0_gnn_in['Wv_l2_c'], 'L0_gnn_Ws_l3': _L0_gnn_in['Ws_l3'], 'L0_gnn_Wv_l3': _L0_gnn_in['Wv_l3']}

def reference(x, src, dst, edge_attr_10, edge_attr_4, node_vec1, node_vec1_n2, node_vec1_n3, L0_gnn_Ws_sc_a, L0_gnn_Wv_sc_a, L0_gnn_Ws_sc_c, L0_gnn_Wv_sc_c, L0_gnn_Ws_l1_a, L0_gnn_Wv_l1_a, L0_gnn_Ws_l1_c, L0_gnn_Wv_l1_c, L0_gnn_W_fc1, L0_gnn_W_fc2, L0_gnn_Ws_l2_a, L0_gnn_Wv_l2_a, L0_gnn_Ws_l2_c, L0_gnn_Wv_l2_c, L0_gnn_Ws_l3, L0_gnn_Wv_l3):
    import jax
    import jax.numpy as jnp

    def _L0_gnn_ref(node_input, node_attr, node_crystal_attr, sym_mask, edge_attr, edge_length_embedded, edge_src, edge_dst, Ws_sc_a, Wv_sc_a, Ws_sc_c, Wv_sc_c, Ws_l1_a, Wv_l1_a, Ws_l1_c, Wv_l1_c, W_fc1, W_fc2, Ws_l2_a, Wv_l2_a, Ws_l2_c, Wv_l2_c, Ws_l3, Wv_l3):
        import jax, jax.numpy as jnp
        import numpy as np
        N = 3125
        E = 50000
        S = 64
        V = 32
        NB = 10
        H = 100
        WN = 192
        MID = 96
        NUM_NEIGHBORS = 16.0
        C_S = float(np.sin(np.pi / 8.0))
        C_X = float(np.cos(np.pi / 8.0))
        SQRT3 = float(np.sqrt(3.0))

        def fctp_scalar_attr(xs, xv, attr, Ws, Wv):
            s = xs * attr @ Ws
            v = jnp.einsum('nuc,uo->noc', xv * attr[:, :, None], Wv)
            return (s, v)
        n = node_input.shape[0]
        xs = node_input[:, :S]
        xv = node_input[:, S:].reshape(n, V, 3)
        ssa, sva = fctp_scalar_attr(xs, xv, node_attr, Ws_sc_a, Wv_sc_a)
        ssc, svc = fctp_scalar_attr(xs, xv, node_crystal_attr, Ws_sc_c, Wv_sc_c)
        s_s, s_v = (ssa + ssc, sva + svc)
        l1a_s, l1a_v = fctp_scalar_attr(xs, xv, node_attr, Ws_l1_a, Wv_l1_a)
        l1c_s, l1c_v = fctp_scalar_attr(xs, xv, node_crystal_attr, Ws_l1_c, Wv_l1_c)
        x1s, x1v = (l1a_s + l1c_s, l1a_v + l1c_v)
        weight = jax.nn.silu(edge_length_embedded @ W_fc1) @ W_fc2
        w0 = weight[:, :S]
        w1 = weight[:, S:2 * S]
        w2 = weight[:, 2 * S:2 * S + V]
        w3 = weight[:, 2 * S + V:]
        gs = x1s[edge_src]
        gv = x1v[edge_src]
        e_s = edge_attr[:, :1]
        e_v = edge_attr[:, 1:]
        mid0a = w0 * gs * e_s
        mid0b = w3 * (jnp.einsum('euc,ec->eu', gv, e_v) / SQRT3)
        mid1a = w1[:, :, None] * gs[:, :, None] * e_v[:, None, :]
        mid1b = w2[:, :, None] * gv * e_s[:, :, None]
        edge_feat = jnp.concatenate([mid0a, mid0b, mid1a.reshape(-1, 3 * S), mid1b.reshape(-1, 3 * V)], axis=-1)
        agg = jax.ops.segment_sum(edge_feat, edge_dst, num_segments=n) / np.sqrt(NUM_NEIGHBORS)
        m_s = agg[:, :MID]
        m_v = agg[:, MID:].reshape(n, MID, 3)
        l2a_s, l2a_v = fctp_scalar_attr(m_s, m_v, node_attr, Ws_l2_a, Wv_l2_a)
        l2c_s, l2c_v = fctp_scalar_attr(m_s, m_v, node_crystal_attr, Ws_l2_c, Wv_l2_c)
        m_s, m_v = (l2a_s + l2c_s, l2a_v + l2c_v)
        o_s, o_v = fctp_scalar_attr(m_s, m_v, sym_mask, Ws_l3, Wv_l3)
        out_s = C_S * s_s + C_X * o_s
        out_v = C_S * s_v + C_X * o_v
        return jnp.concatenate([out_s, out_v.reshape(n, 3 * V)], axis=-1)
    x = _layernorm(x + _L0_gnn_ref(x, node_vec1, node_vec1_n2, node_vec1_n3, edge_attr_4, edge_attr_10, src, dst, L0_gnn_Ws_sc_a, L0_gnn_Wv_sc_a, L0_gnn_Ws_sc_c, L0_gnn_Wv_sc_c, L0_gnn_Ws_l1_a, L0_gnn_Wv_l1_a, L0_gnn_Ws_l1_c, L0_gnn_Wv_l1_c, L0_gnn_W_fc1, L0_gnn_W_fc2, L0_gnn_Ws_l2_a, L0_gnn_Wv_l2_a, L0_gnn_Ws_l2_c, L0_gnn_Wv_l2_c, L0_gnn_Ws_l3, L0_gnn_Wv_l3), axis=-1)
    return x

_drawn_inputs = setup_inputs


def setup_inputs(seed=0):
    import zlib

    import numpy as np

    out = dict(_drawn_inputs(seed))
    spreads = {}
    factors = {}
    for name, (base, spread) in spreads.items():
        noise = np.random.default_rng([zlib.crc32(name.encode()), seed]).standard_normal(out[name].shape)
        drawn = base * np.exp(spread * noise) if base else spread * noise
        out[name] = jnp.asarray(drawn.astype(out[name].dtype))
    for name, factor in factors.items():
        out[name] = (out[name] * factor).astype(out[name].dtype)
    return out
```

```python
from contextlib import ExitStack

import concourse.bass as bass
from concourse import mybir

F32, I32 = mybir.dt.float32, mybir.dt.int32
ALU, ACT, AX = mybir.AluOpType, mybir.ActivationFunctionType, mybir.AxisListType

N, E, S, V, NB, H = 12500, 400000, 64, 32, 10, 100
MID = S + V
D = S + 3 * V
VS = 3 * V
P = 128
NT = -(-N // P)
NP = NT * P
CH = 7
NCH = NT // CH
TILES = E // P
GT = (3, 2)
SUB = sum(GT)
NSUB = 5
ST = SUB * NSUB
NSB = TILES // ST
NG = 2 * NSUB
WIN = 32
SLOTS = NP // WIN
C_S, C_X = 0.3826834323650898, 0.9238795325112867
NEIGHBORS = 16.0
EPS = 1e-5


def prep_phase(nc, q, keep):
    with ExitStack() as ctx:
        sb = lambda name, shape, dt=F32: ctx.enter_context(nc.sbuf_tensor(name, shape, dt))
        sem = lambda name: ctx.enter_context(nc.semaphore(name))
        xTa = [sb(f"xTa{b}", [P, CH * P]) for b in range(2)]
        xTb = [sb(f"xTb{b}", [V, CH * P]) for b in range(2)]
        attrs = [sb(f"attrs{b}", [P, CH, 3]) for b in range(2)]
        wl1a = sb("wl1a", [P, 2 * D])
        wl1b = sb("wl1b", [V, 2 * S])
        part = [sb(f"part{b}", [P, D]) for b in range(2)]
        x1 = [sb(f"x1_{b}", [P, CH, D]) for b in range(2)]
        dst = sb("dst_rows_sb", [NSB, ST * P], I32)
        first, last = sb("first", [NSB, NG]), sb("last", [NSB, NG])
        firsti, sloti = sb("firsti", [NSB, NG], I32), sb("sloti", [NSB, NG], I32)
        span, spani = sb("span", [NSB, NG]), sb("spani", [NSB, NG], I32)
        slotf = sb("slotf", [NSB, NG])
        ftab, itab = sb("ftab_sb", [NSB, 2 * NG]), sb("itab_sb", [NSB, 2 * NG], I32)
        l2T = sb("l2T_sb", [MID, 4 * MID])
        l3 = sb("l3_sb", [MID, S + V])
        rowscale = sb("rowscale", [MID, 1])
        node_ps = [ctx.enter_context(nc.psum_tensor(f"node_ps{b}", [P, 512], F32)) for b in range(2)]
        w3_ps = ctx.enter_context(nc.psum_tensor("w3_ps", [MID, 512], F32))

        weights_in = sem("weights_in")
        x_in = [sem(f"x_in{b}") for b in range(2)]
        dst_in, l_in, chain = sem("dst_in"), sem("l_in"), sem("chain")
        node_mm = sem("node_mm")
        part_done = sem("part_done")
        x1_done = sem("x1_done")
        x1_free = sem("x1_free")
        x1_out = sem("x1_out")
        w3_mm, tab_done, tab_out, scale_set = sem("w3_mm"), sem("tab_done"), sem("tab_out"), sem("scale_set")
        block = ctx.enter_context(nc.Block())

        @block.sync
        def _(sp):
            def load(c, b):
                sp.dma_start(xTa[b][:], q["xT"][0:P, bass.ds(c * (CH * P), CH * P)]).then_inc(x_in[b], 16)
                sp.dma_start(xTb[b][:], q["xT"][P:D, bass.ds(c * (CH * P), CH * P)]).then_inc(x_in[b], 16)
                sp.dma_start(attrs[b][:], q["attrs"][:, bass.ds(c * CH, CH), :]).then_inc(x_in[b], 16)

            sp.dma_start(wl1a[:], q["wl1a"]).then_inc(weights_in, 16)
            sp.dma_start(wl1b[:], q["wl1b"]).then_inc(weights_in, 16)
            for b in range(2):
                load(b, b)
            with sp.Fori(0, NCH // 2 - 1) as i:
                for b in range(2):
                    sp.wait_ge(x1_done, (2 * i + b + 1) * CH + 2)
                    load(2 * i + b + 2, b)

        @block.scalar
        def _(act):
            act.dma_start(dst[:], q["dst_rows"]).then_inc(dst_in, 16)
            for to, of in ((l2T, "l2T"), (l3, "l3"), (keep["wsca"], "wsca"), (keep["wscb"], "wscb"),
                           (keep["iden"], "iden")):
                act.dma_start(to[:], q[of]).then_inc(l_in, 16)
            with act.Fori(0, NCH // 2) as i:
                for u in range(2 * CH):
                    b, t = u // CH, u % CH
                    n = i * (2 * CH) + u
                    act.wait_ge(node_mm, n + 1)
                    act.wait_ge(x1_done, n + 1)
                    nc.scalar.activation(part[u % 2][:], node_ps[u % 2][:, 0:D], ACT.Copy,
                                         scale=attrs[b][:, t, 0:1]).then_inc(part_done, 1)
            act.wait_ge(l_in, 80)
            act.wait_ge(tab_done, 1)
            act.dma_start(q["ftab"], ftab[:]).then_inc(tab_out, 16)
            act.dma_start(q["itab"], itab[:]).then_inc(tab_out, 16)
            act.wait_ge(tab_out, 32)

        @block.tensor
        def _(pe):
            pe.wait_ge(weights_in, 32)
            with pe.Fori(0, NCH // 2) as i:
                for u in range(2 * CH):
                    b, t = u // CH, u % CH
                    n = i * (2 * CH) + u
                    if t == 0:
                        pe.wait_ge(x_in[b], i * 48 + 48)
                    pe.wait_ge(x1_done, n + 1)
                    ps = node_ps[u % 2][:, 0:2 * D]
                    nc.tensor.matmul(ps, xTa[b][:, t * P:(t + 1) * P], wl1a[:], start=True, stop=False,
                                     skip_group_check=True)
                    nc.tensor.matmul(ps.rearrange("p (k d) -> p k d", k=2)[:, :, VS:D],
                                     xTb[b][:, t * P:(t + 1) * P], wl1b[:], start=False, stop=True,
                                     skip_group_check=True).then_inc(node_mm, 1)
            pe.wait_ge(l_in, 80)
            for k in range(2):
                nc.tensor.matmul(w3_ps[:, k * S:(k + 1) * S], l2T[:, k * MID:(k + 1) * MID], l3[:, 0:S],
                                 start=True, stop=True)
            for k in range(2):
                mm = nc.tensor.matmul(w3_ps[:, 2 * S + k * V:2 * S + (k + 1) * V],
                                      l2T[:, (2 + k) * MID:(3 + k) * MID], l3[:, S:], start=True, stop=True)
            mm.then_inc(w3_mm, 1)

        @block.gpsimd
        def _(pool):
            nc.gpsimd.memset(rowscale[0:S, :], 1.0).then_inc(scale_set, 1)
            pool.wait_ge(scale_set, 1)
            nc.gpsimd.memset(rowscale[S:MID, :], float(3.0 ** -0.5)).then_inc(scale_set, 1)
            pool.wait_ge(scale_set, 2)
            nc.gpsimd.iota(keep["iota32"][:], pattern=[[1, WIN]], base=0, channel_multiplier=0,
                           allow_small_or_imprecise_dtypes=True).then_inc(scale_set, 1)
            for blk in range(P // WIN):
                pool.wait_ge(scale_set, 3 + blk)
                nc.gpsimd.iota(keep["iota_row"][blk * WIN:(blk + 1) * WIN, :], pattern=[[1, 1]], base=0,
                               channel_multiplier=1, allow_small_or_imprecise_dtypes=True).then_inc(scale_set, 1)
            pool.wait_ge(scale_set, 3 + P // WIN)
            nc.gpsimd.memset(keep["agg"][:], 0.0)
            with pool.Fori(0, NCH // 2) as i:
                for b in range(2):
                    pool.wait_ge(x1_done, (2 * i + b + 1) * CH + 2)
                    pool.dma_start(q["x1_rows"][:, bass.ds((2 * i + b) * CH, CH), :], x1[b][:]).then_inc(x1_out, 16)
                    pool.wait_ge(x1_out, (2 * i + b + 1) * 16)
                    nc.gpsimd.sem_inc(x1_free, 1)

        @block.vector
        def _(dve):
            links = [0]

            def link(ins):
                links[0] += 1
                ins.then_inc(chain, 1)
                dve.wait_ge(chain, links[0])

            nc.vector.sem_inc(x1_done, 2)
            nc.vector.sem_inc(x1_free, 2)
            with dve.Fori(0, NCH // 2) as i:
                for u in range(2 * CH):
                    b, t = u // CH, u % CH
                    n = i * (2 * CH) + u
                    dve.wait_ge(part_done, n + 1)
                    if t == 0:
                        dve.wait_ge(x1_free, 2 * i + b + 1)
                    nc.vector.scalar_tensor_tensor(
                        x1[b][:, t, :], node_ps[u % 2][:, D:2 * D], attrs[b][:, t, 1:2], part[u % 2][:],
                        ALU.mult, ALU.add).then_inc(x1_done, 1)
            dve.wait_ge(dst_in, 16)
            nodes = dst[:].rearrange("p (s e) -> p s e", s=NSUB)
            for to, op in ((first, ALU.min), (last, ALU.max)):
                kinds = to[:].rearrange("p (s k) -> p s k", k=2)
                nc.vector.tensor_reduce(kinds[:, :, 0:1], nodes[:, :, 0:GT[0] * P], AX.X, op)
                link(nc.vector.tensor_reduce(kinds[:, :, 1:2], nodes[:, :, GT[0] * P:], AX.X, op))
            for to in (first, last):
                link(nc.vector.tensor_scalar(to[:], to[:], 0.0, float(N - 1), ALU.max, ALU.min))
            nc.vector.tensor_copy(firsti[:], first[:])
            link(nc.vector.tensor_tensor(span[:], last[:], first[:], ALU.subtract))
            link(nc.vector.tensor_copy(spani[:], span[:]))
            link(nc.vector.tensor_single_scalar(sloti[:], firsti[:], 5, ALU.arith_shift_right))
            nc.vector.tensor_single_scalar(itab[:, NG:], spani[:], 5, ALU.arith_shift_right)
            link(nc.vector.tensor_copy(slotf[:], sloti[:]))
            nc.vector.tensor_copy(ftab[:, 0:NG], first[:])
            nc.vector.tensor_scalar(ftab[:, NG:], slotf[:], float(WIN), None, ALU.mult)
            nc.vector.tensor_scalar(itab[:, 0:NG], slotf[:], float(MID), None, ALU.mult).then_inc(tab_done, 1)
            dve.wait_ge(w3_mm, 1)
            dve.wait_ge(scale_set, 2)
            nc.vector.tensor_scalar(keep["w3s"][:], w3_ps[:, 0:2 * S], rowscale[:], None, ALU.mult)
            nc.vector.tensor_copy(keep["w3v"][:], w3_ps[:, 2 * S:2 * S + 2 * V])


def edge_phase(nc, q, keep):
    with ExitStack() as ctx:
        sb = lambda name, shape, dt=F32: ctx.enter_context(nc.sbuf_tensor(name, shape, dt))
        ps = lambda name, cols: ctx.enter_context(nc.psum_tensor(name, [P, cols], F32))
        sem = lambda name: ctx.enter_context(nc.semaphore(name))
        agg = keep["agg"]
        w1 = sb("w1", [P, NSUB * H])
        w2 = sb("w2", [H, 2 * MID])
        rows_at = keep["iden"]
        src = [sb(f"src{b}", [P, ST], I32) for b in range(2)]
        dsti = [sb(f"dsti{b}", [P, ST], I32) for b in range(2)]
        ea = [sb(f"ea{b}", [P, ST, 4]) for b in range(2)]
        tab = [sb(f"tab{b}", [P, 2 * NG]) for b in range(2)]
        regs_row = [sb(f"regs_row{b}", [1, 2 * NG], I32) for b in range(2)]
        elen = [sb(f"elen{b}", [P, SUB * P]) for b in range(2)]
        gat = sb("gat", [P, ST, D])
        hid = [sb(f"hid{k}", [H, GT[k] * P]) for k in range(2)]
        feat = [sb(f"feat{k}", [P, GT[k], 2, D]) for k in range(2)]
        hot = [sb(f"hot{k}", [P, GT[k], WIN]) for k in range(2)]
        sel = [sb(f"sel{k}", [P, GT[k], 4, WIN]) for k in range(2)]
        dstf = sb("dstf", [P, ST])
        rel = [sb(f"rel{b}", [P, ST]) for b in range(2)]
        off = [sb(f"off{b}", [P, ST]) for b in range(2)]
        wrap, beyond = sb("wrap", [P, ST]), sb("beyond", [P, ST])
        row = [sb(f"row{b}", [P, ST]) for b in range(2)]
        m = sb("m", [P, NG])
        keep_lo = [sb(f"keep_lo{b}", [P, NG]) for b in range(2)]
        keep_hi = [sb(f"keep_hi{b}", [P, NG]) for b in range(2)]
        stage = [sb(f"stage{k}", [P, VS]) for k in range(2)]
        xrel, xoff, xrow, xa = sb("xrel", [P, GT[0]]), sb("xoff", [P, GT[0]]), sb("xrow", [P, GT[0]]), sb("xa", [P, GT[0]])
        xhot = sb("xhot", [P, GT[0], WIN])
        xsel = sb("xsel", [P, GT[0], 4, WIN])
        xstage = sb("xstage", [P, VS])

        hid_ps = [ps(f"hid_ps{k}", 512) for k in range(2)]
        wgt_ps = [ps("wgt_ps0", 1024), ps("wgt_ps1", 512)]
        win_ps = [ps(f"win_ps{k}", 512) for k in range(2)]
        xwin_ps = ps("xwin_ps", 512)

        const_in, w1_zero = sem("const_in"), sem("w1_zero")
        src_in = [sem(f"src_in{b}") for b in range(2)]
        edge_in = [sem(f"edge_in{b}") for b in range(2)]
        row_in = [sem(f"row_in{b}") for b in range(2)]
        len_in = [sem(f"len_in{b}") for b in range(2)]
        gat_in = [sem(f"gat_in{j}") for j in range(NG)]
        hid_mm = sem("hid_mm")
        silu_done = sem("silu_done")
        wgt_mm = sem("wgt_mm")
        feat_done = sem("feat_done")
        sel_done = sem("sel_done")
        win_mm = sem("win_mm")
        stage_done = sem("stage_done")
        swap_mm = sem("swap_mm")
        agg_done = sem("agg_done")
        slots_seen, counts_read = sem("slots_seen"), sem("counts_read")
        row_seen = sem("row_seen")
        hot_done, prep, rows_done = sem("hot_done"), sem("prep"), sem("rows_done")
        x_ready, x_win, x_stage, x_swap, x_chain = (sem(n) for n in ("x_ready", "x_win", "x_stage", "x_swap", "x_chain"))
        block = ctx.enter_context(nc.Block())

        def tile0(j):
            return (j // 2) * SUB + (j % 2) * GT[0]

        @block.sync
        def _(sp):
            def load(n, b):
                row0 = bass.ds(n, 1)
                sp.dma_start(src[b][:], q["src_cols"][row0].rearrange("a p t -> p (a t)")).then_inc(src_in[b], 16)
                sp.dma_start(dsti[b][:], q["dst_cols"][row0].rearrange("a p t -> p (a t)")).then_inc(edge_in[b], 16)
                sp.dma_start(ea[b][:].rearrange("p t c -> p (t c)"),
                             q["ea"][row0].rearrange("a p t -> p (a t)")).then_inc(edge_in[b], 16)
                sp.dma_start(tab[b][:], q["ftab"][row0, :].to_broadcast([P, 2 * NG])).then_inc(edge_in[b], 16)
                sp.dma_start(regs_row[b][:], q["itab"][row0, :]).then_inc(row_in[b], 16)
                sp.dma_start(elen[b][0:NSUB * NB, :],
                             q["elen"][row0].rearrange("a p e -> p (a e)")).then_inc(len_in[b], 16)

            sp.dma_start(w2[:], q["w2"]).then_inc(const_in, 16)
            sp.wait_ge(w1_zero, 3)
            for s in range(NSUB):
                sp.dma_start(w1[s * NB:(s + 1) * NB, s * H:(s + 1) * H], q["w1"]).then_inc(const_in, 16)
            for b in range(2):
                load(b, b)
            with sp.Fori(0, (NSB - 3) // 2) as i:
                for b in range(2):
                    sp.wait_ge(agg_done, (2 * i + b + 1) * NG + 2)
                    sp.wait_ge(counts_read, 2 * i + b + 1)
                    load(2 * i + b + 2, b)
            sp.wait_ge(agg_done, (NSB - 2) * NG + 2)
            sp.wait_ge(counts_read, NSB - 2)
            load(NSB - 1, 0)

        def superblocks(eng, body):
            with eng.Fori(0, NSB // 2) as i:
                for b in range(2):
                    body(2 * i + b, i, b, False)
            body(NSB - 1, NSB // 2, 0, True)

        @block.gpsimd
        def _(pool):
            nc.gpsimd.memset(w1[:], 0.0).then_inc(w1_zero, 1)
            for b in range(2):
                nc.gpsimd.memset(elen[b][:], 0.0).then_inc(w1_zero, 1)

            def body(n, i, b, last):
                pool.wait_ge(src_in[b], i * 16 + 16)
                for j in range(NG):
                    pool.wait_ge(feat_done, n * NG + j + 1)
                    nc.gpsimd.sem_inc(slots_seen, 1)
                    for t in range(tile0(j), tile0(j) + GT[j % 2]):
                        nc.gpsimd.indirect_dma_start(
                            out=gat[:, t, :], out_offset=None, in_=q["x1"],
                            in_offset=bass.IndirectOffsetOnAxis(ap=src[b][:, t:t + 1], axis=0)
                        ).then_inc(gat_in[j], 16)
            superblocks(pool, body)

        @block.scalar
        def _(act):
            nc.scalar.sem_inc(silu_done, 2)

            def silu(g, k):
                act.wait_ge(hid_mm, g + 1)
                act.wait_ge(wgt_mm, g + 1)
                nc.scalar.activation(hid[k][:], hid_ps[k][0:H, 0:GT[k] * P], ACT.Silu).then_inc(silu_done, 1)

            def body(n, i, b, last):
                for j in range(NG):
                    g, k = n * NG + j, j % 2
                    act.wait_ge(win_mm, g + 3)
                    act.wait_ge(swap_mm, g + 1)
                    nc.scalar.activation(stage[k][:], win_ps[k][:, 0:VS], ACT.Copy).then_inc(stage_done, 1)
                    if not (last and j + 3 >= NG):
                        silu(g + 3, (j + 3) % 2)
            for g in range(3):
                silu(g, g % 2)
            superblocks(act, body)

        @block.tensor
        def _(pe):
            nc.tensor.sem_inc(wgt_mm, 2)
            nc.tensor.sem_inc(win_mm, 2)
            nc.tensor.sem_inc(swap_mm, 2)
            extra_regs = [pe.alloc_register(f"pe_extra{j}") for j in range(NG)]
            count = pe.alloc_register("pe_count")
            pe.reg_mov(count, 0)
            pe.wait_ge(const_in, 16 * (1 + NSUB))

            def hidden(g, j, b, i):
                k = j % 2
                if j == 0:
                    pe.wait_ge(len_in[b], i * 16 + 16)
                pe.wait_ge(silu_done, g + 1)
                nc.tensor.matmul(hid_ps[k][0:H, 0:GT[k] * P], w1[:, (j // 2) * H:(j // 2 + 1) * H],
                                 elen_of(b, j), start=True, stop=True).then_inc(hid_mm, 1)

            def elen_of(b, j):
                c0 = (j % 2) * GT[0] * P
                return elen[b][:, c0:c0 + GT[j % 2] * P]

            def weights(g, k):
                pe.wait_ge(silu_done, g + 3)
                pe.wait_ge(feat_done, g + NG - 1)
                for t in range(GT[k]):
                    mm = nc.tensor.matmul(wgt_ps[k][:, t * 256:t * 256 + 2 * MID], hid[k][:, t * P:(t + 1) * P],
                                          w2[:], start=True, stop=True)
                mm.then_inc(wgt_mm, 1)

            def window(to, one_hot, k):
                for t in range(GT[k]):
                    for c in range(4):
                        mm = nc.tensor.matmul(to[c * WIN:(c + 1) * WIN, 0:D], one_hot[:, t, c, :],
                                              feat[k][:, t, min(c, 1), :], start=t == 0, stop=t == GT[k] - 1,
                                              tile_position=(0, c * WIN))
                return mm

            def swapped(to, of):
                for c in range(3):
                    columns = of[:, c * V:(c + 1) * V]
                    there = (c + 1) * WIN
                    nc.tensor.matmul(to[there:there + WIN, D:D + V], rows_at[:, 0:WIN], columns, start=True, stop=True,
                                     tile_position=(0, there))
                    mm = nc.tensor.matmul(to[0:WIN, D:D + V], rows_at[:, there:there + WIN], columns, start=c == 0,
                                          stop=c == 2, tile_position=(0, 0))
                return mm

            def window_of(g, k):
                pe.wait_ge(feat_done, g + NG + 1)
                pe.wait_ge(sel_done, g + 1)
                pe.wait_ge(agg_done, g + 1)
                window(win_ps[k], sel[k], k).then_inc(win_mm, 1)

            def more_windows(k, extra):
                with pe.If(extra > 0):
                    with pe.Fori(0, extra) as _w:
                        pe.reg_add(count, count, 1)
                        pe.wait_ge(x_ready, pe.snap(count))
                        window(xwin_ps, xsel, k).then_inc(x_win, 1)
                        pe.wait_ge(x_stage, pe.snap(count))
                        swapped(xwin_ps, xstage).then_inc(x_swap, 1)

            hidden(0, 0, 0, 0)
            hidden(1, 1, 0, 0)
            weights(0, 0)
            hidden(2, 2, 0, 0)
            weights(1, 1)
            window_of(0, 0)

            def body(n, i, b, last):
                pe.wait_ge(row_in[b], i * 16 + 16)
                nc.tensor.sem_inc(row_seen, 1)
                pe.reg_load(extra_regs, regs_row[b][0:1, NG:])
                nc.tensor.sem_inc(counts_read, 1)
                for j in range(NG):
                    g, k = n * NG + j, j % 2
                    more_windows(k, pe.snap(extra_regs[j], min_val=0, max_val=SLOTS))
                    if not (last and j + 2 >= NG):
                        weights(g + 2, k)
                    if not (last and j + 3 >= NG):
                        over = j + 3 >= NG
                        hidden(g + 3, (j + 3) % NG, (b + 1) % 2 if over else b, i + b if over else i)
                    if not (last and j + 1 >= NG):
                        window_of(g + 1, 1 - k)
                    pe.wait_ge(stage_done, g + 1)
                    swapped(win_ps[k], stage[k]).then_inc(swap_mm, 1)
            superblocks(pe, body)

        @block.vector
        def _(dve):
            nc.vector.sem_inc(feat_done, NG)
            nc.vector.sem_inc(agg_done, 2)
            slot_regs = [dve.alloc_register(f"dve_slot{j}") for j in range(NG)]
            extra_regs = [dve.alloc_register(f"dve_extra{j}") for j in range(NG)]
            count = dve.alloc_register("dve_count")
            dve.reg_mov(count, 0)
            PREP = 4

            def kinds(ap):
                v = ap.rearrange("p (s t) -> p s t", t=SUB)
                return v[:, :, 0:GT[0]], v[:, :, GT[0]:]

            def rows(n, i, b):
                dve.wait_ge(edge_in[b], i * 48 + 48)
                first = tab[b][:, 0:NG].rearrange("p (s k) -> p s k", k=2)
                slot0 = tab[b][:, NG:].rearrange("p (s k) -> p s k", k=2)
                nc.vector.tensor_copy(dstf[:], dsti[b][:])
                nc.vector.tensor_tensor(m[:], tab[b][:, 0:NG], tab[b][:, NG:], ALU.subtract).then_inc(prep, 1)
                dve.wait_ge(prep, n * PREP + 1)
                for k in range(2):
                    shape = [P, NSUB, GT[k]]
                    nc.vector.tensor_tensor(kinds(rel[b][:])[k], kinds(dstf[:])[k],
                                            first[:, :, k:k + 1].to_broadcast(shape), ALU.subtract)
                    nc.vector.tensor_tensor(kinds(off[b][:])[k], kinds(dstf[:])[k],
                                            slot0[:, :, k:k + 1].to_broadcast(shape), ALU.subtract)
                nc.vector.tensor_scalar(keep_lo[b][:], m[:], keep["iota_row"][:], None, ALU.is_le)
                nc.vector.tensor_scalar(keep_hi[b][:], m[:], keep["iota_row"][:], None, ALU.is_gt).then_inc(prep, 1)
                dve.wait_ge(prep, n * PREP + 2)
                nc.vector.tensor_scalar(wrap[:], off[b][:], float(WIN), -float(WIN), ALU.is_ge, ALU.mult)
                nc.vector.tensor_scalar(beyond[:], rel[b][:], float(WIN), 1000.0, ALU.is_ge, ALU.mult).then_inc(prep, 1)
                dve.wait_ge(prep, n * PREP + 3)
                nc.vector.tensor_tensor(wrap[:], wrap[:], beyond[:], ALU.add).then_inc(prep, 1)
                dve.wait_ge(prep, n * PREP + 4)
                nc.vector.tensor_tensor(row[b][:], off[b][:], wrap[:], ALU.add).then_inc(rows_done, 1)
                dve.wait_ge(rows_done, n + 1)

            def one_hot(to, rows_of, k):
                shape = [P, GT[k], WIN]
                return nc.vector.tensor_tensor(to[:, 0:GT[k], :], keep["iota32"][:, None, :].to_broadcast(shape),
                                               rows_of[:, :, None].to_broadcast(shape), ALU.is_equal)

            def scaled(to, hots, b, t0, k):
                shape = [P, GT[k], 4, WIN]
                return nc.vector.tensor_tensor(to[:, 0:GT[k]], hots[:, 0:GT[k], None, :].to_broadcast(shape),
                                               ea[b][:, t0:t0 + GT[k], :, None].to_broadcast(shape), ALU.mult)

            def block_of(g, n, i, b, j):
                k, t0 = j % 2, tile0(j)
                if j == 0:
                    rows(n, i, b)
                dve.wait_ge(win_mm, g + 1)
                one_hot(hot[k], row[b][:, t0:t0 + GT[k]], k).then_inc(hot_done, 1)
                dve.wait_ge(wgt_mm, g + 3)
                dve.wait_ge(gat_in[j], n * (16 * GT[k]) + 16 * GT[k])
                T = GT[k]
                w = wgt_ps[k][:].rearrange("p (t c) -> p t c", c=256)[:, 0:T, :]
                rows_g = gat[:, t0:t0 + T, :]
                nc.vector.tensor_tensor(
                    feat[k][:, :, :, VS:D], w[:, :, 0:2 * S].rearrange("p t (h s) -> p t h s", h=2),
                    rows_g[:, :, None, VS:D].to_broadcast([P, T, 2, S]), ALU.mult)
                for h in range(2):
                    f = nc.vector.tensor_tensor(
                        feat[k][:, :, h, 0:VS].rearrange("p t (c u) -> p t c u", c=3),
                        w[:, :, None, 2 * S + h * V:2 * S + (h + 1) * V].to_broadcast([P, T, 3, V]),
                        rows_g[:, :, 0:VS].rearrange("p t (c u) -> p t c u", c=3), ALU.mult)
                f.then_inc(feat_done, 1)
                dve.wait_ge(hot_done, g + 1)
                scaled(sel[k], hot[k], b, t0, k).then_inc(sel_done, 1)

            def add_window(win, col, b, j):
                for half, mask in ((0, keep_lo), (1, keep_hi)):
                    to = agg[:, bass.ds(col + half * MID, MID)]
                    last = nc.vector.scalar_tensor_tensor(to, win[:, VS:D + V], mask[b][:, j:j + 1], to,
                                                          ALU.mult, ALU.add)
                return last

            def more_windows(b, j, extra):
                k, t0 = j % 2, tile0(j)
                T = GT[k]
                tiles = slice(t0, t0 + T)
                with dve.If(extra > 0):
                    nc.vector.tensor_copy(xrel[:, 0:T], rel[b][:, tiles])
                    nc.vector.tensor_copy(xoff[:, 0:T], off[b][:, tiles])
                    nc.vector.drain()
                    with dve.Fori(0, extra) as _w:
                        dve.reg_add(count, count, 1)
                        dve.reg_add(slot_regs[j], slot_regs[j], MID)
                        for a in (xrel, xoff):
                            nc.vector.tensor_scalar(a[:, 0:T], a[:, 0:T], -float(WIN), None, ALU.add)
                        nc.vector.drain()
                        for of, lim, op, val in ((xoff, float(WIN), ALU.is_ge, -float(WIN)),
                                                 (xrel, float(WIN), ALU.is_ge, 1000.0),
                                                 (xrel, 0.0, ALU.is_lt, 1000.0)):
                            nc.vector.tensor_scalar(xa[:, 0:T], of[:, 0:T], lim, val, op, ALU.mult)
                            nc.vector.drain()
                            nc.vector.tensor_tensor(xrow[:, 0:T], xoff[:, 0:T] if of is xoff else xrow[:, 0:T],
                                                    xa[:, 0:T], ALU.add)
                            nc.vector.drain()
                        one_hot(xhot, xrow[:, 0:T], k)
                        nc.vector.drain()
                        scaled(xsel, xhot, b, t0, k).then_inc(x_ready, 1)
                        dve.wait_ge(x_win, dve.snap(count))
                        nc.vector.tensor_copy(xstage[:], xwin_ps[:, 0:VS]).then_inc(x_stage, 1)
                        dve.wait_ge(x_swap, dve.snap(count))
                        add_window(xwin_ps, dve.snap(slot_regs[j], min_val=0, max_val=(SLOTS - 2) * MID), b, j)
                        nc.vector.drain()

            def body(n, i, b, last):
                dve.wait_ge(row_in[b], i * 16 + 16)
                nc.vector.sem_inc(row_seen, 1)
                dve.reg_load(slot_regs + extra_regs, regs_row[b][0:1, :])
                for j in range(NG):
                    g = n * NG + j
                    col = dve.snap(slot_regs[j], min_val=0, max_val=(SLOTS - 2) * MID)
                    more_windows(b, j, dve.snap(extra_regs[j], min_val=0, max_val=SLOTS))
                    if not (last and j + 2 >= NG):
                        if j + 2 < NG:
                            block_of(g + 2, n, i, b, j + 2)
                        else:
                            block_of(g + 2, n + 1, i + b, (b + 1) % 2, j + 2 - NG)
                    dve.wait_ge(swap_mm, g + 3)
                    dve.wait_ge(agg_done, g + 2)
                    add_window(win_ps[j % 2], col, b, j).then_inc(agg_done, 1)

            block_of(0, 0, 0, 0, 0)
            block_of(1, 0, 0, 0, 1)
            superblocks(dve, body)


def node_phase(nc, q, keep):
    with ExitStack() as ctx:
        sb = lambda name, shape, dt=F32: ctx.enter_context(nc.sbuf_tensor(name, shape, dt))
        psum = lambda name: ctx.enter_context(nc.psum_tensor(name, [P, 512], F32))
        sem = lambda name: ctx.enter_context(nc.semaphore(name))
        agg = keep["agg"]
        W4 = P // WIN
        xTa = [sb(f"n_xTa{b}", [P, CH * P]) for b in range(2)]
        xTb = [sb(f"n_xTb{b}", [V, CH * P]) for b in range(2)]
        attrs = [sb(f"n_attrs{b}", [P, CH, 3]) for b in range(2)]
        res = [sb(f"res{b}", [P, CH, D]) for b in range(2)]
        scales = [sb(f"scales{b}", [P, CH, 4]) for b in range(2)]
        packed = [sb(f"packed{b}", [P, W4 * MID]) for b in range(2)]
        aggT = [sb(f"aggT{b}", [MID, 4, P]) for b in range(2)]
        stats = [sb(f"stats{b}", [P, 6]) for b in range(2)]
        moments = [sb(f"moments{b}", [P, CH, 2]) for b in range(2)]
        rstd = [sb(f"rstd{b}", [P, CH]) for b in range(2)]
        shift = [sb(f"shift{b}", [P, CH]) for b in range(2)]
        epst = sb("epst", [P, 1])
        turn_ps = [psum(f"turn_ps{b}") for b in range(2)]
        self_ps = [psum(f"self_ps{b}") for b in range(2)]
        out_ps = [psum(f"out_ps{b}") for b in range(2)]

        x_in = [sem(f"n_x_in{b}") for b in range(2)]
        packed_done = sem("packed_done")
        turn_mm = sem("turn_mm")
        turned = sem("turned")
        self_mm = sem("self_mm")
        out_mm = sem("out_mm")
        sum_done = sem("sum_done")
        chain, tail, tail2 = sem("n_chain"), sem("tail"), sem("tail2")
        std_done, shift_done, norm_done, stored = sem("std_done"), sem("shift_done"), sem("norm_done"), sem("stored")
        free = sem("n_free")
        eps_set = sem("eps_set")
        block = ctx.enter_context(nc.Block())

        def chunks(eng, body):
            with eng.Fori(0, NCH // 2) as i:
                for b in range(2):
                    body(2 * i + b, i, b)

        @block.sync
        def _(sp):
            def load(c, b):
                sp.dma_start(xTa[b][:], q["xT"][0:P, bass.ds(c * (CH * P), CH * P)]).then_inc(x_in[b], 16)
                sp.dma_start(xTb[b][:], q["xT"][P:D, bass.ds(c * (CH * P), CH * P)]).then_inc(x_in[b], 16)
                sp.dma_start(attrs[b][:], q["attrs"][:, bass.ds(c * CH, CH), :]).then_inc(x_in[b], 16)
                sp.dma_start(res[b][:], q["x_rows"][:, bass.ds(c * CH, CH), :]).then_inc(x_in[b], 16)

            def store(c, b):
                sp.wait_ge(norm_done, (c + 1) * CH)
                sp.dma_start(q["out_rows"][:, bass.ds(c * CH, CH), :], res[b][:]).then_inc(stored, 16)
                sp.wait_ge(stored, (c + 1) * 16)

            for b in range(2):
                load(b, b)
            with sp.Fori(0, NCH // 2 - 1) as i:
                for b in range(2):
                    store(2 * i + b, b)
                    load(2 * i + b + 2, b)
            for b in range(2):
                store(NCH - 2 + b, b)

        @block.gpsimd
        def _(pool):
            nc.gpsimd.memset(epst[:], EPS).then_inc(eps_set, 1)

            def body(c, i, b):
                for t in range(CH):
                    u = b * CH + t
                    n = i * (2 * CH) + u
                    pool.wait_ge(turn_mm, n + 1)
                    nc.gpsimd.tensor_copy(packed[u % 2][:], agg[:, bass.ds(n * (W4 * MID), W4 * MID)]
                                          ).then_inc(packed_done, 1)
            chunks(pool, body)

        @block.tensor
        def _(pe):
            nc.tensor.sem_inc(turn_mm, 2)
            nc.tensor.sem_inc(out_mm, 2)

            def body(c, i, b):
                pe.wait_ge(x_in[b], i * 64 + 64)
                for t in range(CH):
                    u = b * CH + t
                    n = i * (2 * CH) + u
                    pe.wait_ge(packed_done, n + 1)
                    pe.wait_ge(turned, n + 1)
                    for w in range(W4):
                        mm = nc.tensor.transpose(turn_ps[u % 2][0:MID, w * P:(w + 1) * P],
                                                 packed[u % 2][:, w * MID:(w + 1) * MID], keep["iden"][:])
                    mm.then_inc(turn_mm, 1)
                    pe.wait_ge(sum_done, n + 1)
                    ps = self_ps[u % 2][:, 0:2 * D]
                    nodes = slice(t * P, (t + 1) * P)
                    nc.tensor.matmul(ps, xTa[b][:, nodes], keep["wsca"][:], start=True, stop=False,
                                     skip_group_check=True)
                    nc.tensor.matmul(ps.rearrange("p (k d) -> p k d", k=2)[:, :, VS:D], xTb[b][:, nodes],
                                     keep["wscb"][:], start=False, stop=True, skip_group_check=True
                                     ).then_inc(self_mm, 1)
                    pe.wait_ge(turned, n + 3)
                    po = out_ps[u % 2][:, 0:2 * D].rearrange("p (k d) -> p k d", k=2)
                    nc.tensor.matmul(po[:, :, VS:D], aggT[u % 2][:, 0, :], keep["w3s"][:], start=True, stop=True,
                                     skip_group_check=True)
                    for v in range(3):
                        mm = nc.tensor.matmul(po[:, :, v * V:(v + 1) * V], aggT[u % 2][:, 1 + v, :], keep["w3v"][:],
                                              start=False, stop=True, skip_group_check=True)
                    mm.then_inc(out_mm, 1)
            chunks(pe, body)

        @block.scalar
        def _(act):
            nc.scalar.sem_inc(turned, 2)
            act.wait_ge(eps_set, 1)

            def body(c, i, b):
                for t in range(CH):
                    u = b * CH + t
                    n = i * (2 * CH) + u
                    act.wait_ge(turn_mm, n + 3)
                    act.wait_ge(out_mm, n + 1)
                    nc.scalar.activation(aggT[u % 2][:].rearrange("m q (w r) -> m w q r", w=W4),
                                         turn_ps[u % 2][0:MID, :].rearrange("m (w q r) -> m w q r", w=W4, q=4),
                                         ACT.Copy).then_inc(turned, 1)
                act.wait_ge(tail, c + 1)
                nc.scalar.activation(rstd[b][:], moments[b][:, :, 1], ACT.Sqrt, bias=epst[:]).then_inc(std_done, 1)
                act.wait_ge(shift_done, c + 1)
                for t in range(CH):
                    nc.scalar.activation(res[b][:, t, :], res[b][:, t, :], ACT.Identity, scale=rstd[b][:, t:t + 1],
                                         bias=shift[b][:, t:t + 1]).then_inc(norm_done, 1)
            chunks(act, body)

        @block.vector
        def _(dve):
            nc.vector.sem_inc(sum_done, 2)

            def body(c, i, b):
                dve.wait_ge(x_in[b], i * 64 + 64)
                nc.vector.tensor_scalar(scales[b][:, :, 0:2], attrs[b][:, :, 0:2], C_S, None, ALU.mult)
                nc.vector.scalar_tensor_tensor(scales[b][:, :, 2:4], attrs[b][:, :, 0:2], C_X / NEIGHBORS ** 0.5,
                                               attrs[b][:, :, 2:3].to_broadcast([P, CH, 2]), ALU.mult, ALU.mult
                                               ).then_inc(chain, 1)
                for t in range(CH):
                    u = b * CH + t
                    n = i * (2 * CH) + u
                    x = res[b][:, t, :]
                    steps = c * (4 * CH) + 4 * t + c + 1
                    dve.wait_ge(self_mm, n + 1)
                    for h in range(4):
                        dve.wait_ge(chain, steps + h)
                        if h == 2:
                            dve.wait_ge(out_mm, n + 3)
                        of = self_ps if h < 2 else out_ps
                        s = nc.vector.scalar_tensor_tensor(x, of[u % 2][:, (h % 2) * D:(h % 2 + 1) * D],
                                                           scales[b][:, t, h:h + 1], x, ALU.mult, ALU.add
                                                           ).then_inc(chain, 1)
                    dve.wait_ge(chain, steps + 4)
                    nc.vector.bn_stats(stats[u % 2][:], x).then_inc(sum_done, 1)
                    nc.vector.drain()
                    agg_ins = nc.vector.bn_aggr(moments[b][:, t, :], stats[u % 2][:])
                agg_ins.then_inc(tail, 1)
                dve.wait_ge(std_done, c + 1)
                nc.vector.reciprocal(rstd[b][:], rstd[b][:]).then_inc(tail2, 1)
                dve.wait_ge(tail2, c + 1)
                nc.vector.scalar_tensor_tensor(shift[b][:], moments[b][:, :, 0], -1.0, rstd[b][:], ALU.mult, ALU.mult
                                               ).then_inc(shift_done, 1)
            chunks(dve, body)


def build(nc, a, out):
    q = dict(a)
    x1 = nc.dram_tensor("x1", [NP, D], F32, kind="Internal").ap()
    q["x1"] = x1
    q["x1_rows"] = x1.rearrange("(t p) d -> p t d", p=P)
    q["x_rows"] = a["x"].rearrange("(t p) d -> p t d", p=P)
    q["out_rows"] = out.rearrange("(t p) d -> p t d", p=P)
    q["ftab"] = nc.dram_tensor("ftab", [NSB, 2 * NG], F32, kind="Internal").ap()
    q["itab"] = nc.dram_tensor("itab", [NSB, 2 * NG], I32, kind="Internal").ap()
    with ExitStack() as ctx:
        sb = lambda name, shape: ctx.enter_context(nc.sbuf_tensor(name, shape, F32))
        keep = {
            "agg": sb("agg", [P, SLOTS * MID]),
            "iota32": sb("iota32", [P, WIN]), "iota_row": sb("iota_row", [P, 1]),
            "wsca": sb("wsca_sb", [P, 2 * D]), "wscb": sb("wscb_sb", [V, 2 * S]), "iden": sb("iden_sb", [P, P]),
            "w3s": sb("w3s", [MID, 2 * S]), "w3v": sb("w3v", [MID, 2 * V]),
        }
        prep_phase(nc, q, keep)
        edge_phase(nc, q, keep)
        node_phase(nc, q, keep)


def kernel(**inputs):
    import numpy as np
    import concourse.bacc as bacc
    from concourse.bass_utils import run_bass_kernel_spmd as run

    a = {k: np.asarray(v) for k, v in inputs.items()}
    w = {k[len("L0_gnn_"):]: v for k, v in a.items() if k.startswith("L0_gnn_")}

    def columns(x):
        v = x[:, S:].reshape(-1, V, 3).transpose(0, 2, 1).reshape(-1, VS)
        return np.concatenate([v, x[:, :S]], axis=1)

    def padded(x):
        out = np.zeros((NP,) + x.shape[1:], x.dtype)
        out[:N] = x
        return out

    def diagonal(kind):
        out = np.zeros((D, 2, D), np.float32)
        for h, name in enumerate("ac"):
            for c in range(3):
                out[c * V:(c + 1) * V, h, c * V:(c + 1) * V] = w[f"Wv_{kind}_{name}"]
            out[VS:, h, VS:] = w[f"Ws_{kind}_{name}"]
        return out[:P].reshape(P, 2 * D), out[P:, :, VS:].reshape(V, 2 * S)

    xp = padded(columns(a["x"]))
    attrs = np.stack([padded(a[k][:, 0]) for k in ("node_vec1", "node_vec1_n2", "node_vec1_n3")], axis=1)
    l1, sc = diagonal("l1"), diagonal("sc")
    arrays = {
        "x": xp, "xT": xp.T, "attrs": attrs.reshape(NT, P, 3).transpose(1, 0, 2),
        "src_cols": a["src"].reshape(NSB, ST, P).transpose(0, 2, 1),
        "dst_cols": a["dst"].reshape(NSB, ST, P).transpose(0, 2, 1),
        "dst_rows": a["dst"].reshape(NSB, ST * P),
        "ea": a["edge_attr_4"].reshape(NSB, ST, P, 4).transpose(0, 2, 1, 3).reshape(NSB, P, ST * 4),
        "elen": a["edge_attr_10"].reshape(NSB, NSUB, SUB * P, NB).transpose(0, 1, 3, 2).reshape(NSB, NSUB * NB, SUB * P),
        "wl1a": l1[0], "wl1b": l1[1], "wsca": sc[0], "wscb": sc[1],
        "w1": w["W_fc1"], "w2": w["W_fc2"],
        "l2T": np.stack([w[k].T for k in ("Ws_l2_a", "Ws_l2_c", "Wv_l2_a", "Wv_l2_c")], axis=1).reshape(MID, 4 * MID),
        "l3": np.concatenate([w["Ws_l3"], w["Wv_l3"]], axis=1),
        "iden": np.eye(P, dtype=np.float32),
    }
    nc = bacc.Bacc("TRN2", target_bir_lowering=False, num_devices=1)
    aps, feed = {}, {}
    for name, x in arrays.items():
        feed[f"in_{name}"] = np.ascontiguousarray(x)
        aps[name] = nc.dram_tensor(f"in_{name}", x.shape, mybir.dt.from_np(x.dtype), kind="ExternalInput").ap()
    out = nc.dram_tensor("out_0", (NP, D), F32, kind="ExternalOutput").ap()
    build(nc, aps, out)
    got = run(nc, [feed], core_ids=[0]).results[0]["out_0"][:N]
    return np.concatenate([got[:, VS:], got[:, :VS].reshape(N, 3, V).transpose(0, 2, 1).reshape(N, VS)], axis=1)
```

```python
from contextlib import ExitStack

import concourse.bass as bass
from concourse import mybir

F32, BF16, I32 = mybir.dt.float32, mybir.dt.bfloat16, mybir.dt.int32
ALU, ACT, AX = mybir.AluOpType, mybir.ActivationFunctionType, mybir.AxisListType

N, E, S, V, NB, H = 12500, 400000, 64, 32, 10, 100
MID = S + V
D = S + 3 * V
VS = 3 * V
P = 128
NT = -(-N // P)
NP = NT * P
CH = 7
NCH = NT // CH
TILES = E // P
GT = (3, 2)
SUB = sum(GT)
NSUB = 5
ST = SUB * NSUB
NSB = TILES // ST
NG = 2 * NSUB
WIN = 32
SLOTS = NP // WIN
W_ROWS = NB * 6
RAW = NB * ST * P // P
AHEAD = 3
C_S, C_X = 0.3826834323650898, 0.9238795325112867
NEIGHBORS = 16.0
EPS = 1e-5


def prep_phase(nc, q, keep):
    with ExitStack() as ctx:
        sb = lambda name, shape, dt=F32: ctx.enter_context(nc.sbuf_tensor(name, shape, dt))
        sem = lambda name: ctx.enter_context(nc.semaphore(name))
        NBUF = CH
        vT = [sb(f"vT{b}", [P, CH * P]) for b in range(2)]
        sT = [sb(f"sT{b}", [S, CH * P]) for b in range(2)]
        wv, ws = sb("wv_l1", [P, 2 * VS]), sb("ws_l1", [S, 2 * S])
        part = [sb(f"part{b}", [P, D]) for b in range(NBUF)]
        x1 = [sb(f"x1_{b}", [P, CH, D]) for b in range(2)]
        dst = sb("dst_rows_sb", [NSB, ST * P], I32)
        first, last = sb("first", [NSB, NG]), sb("last", [NSB, NG])
        firsti, sloti = sb("firsti", [NSB, NG], I32), sb("sloti", [NSB, NG], I32)
        span, spani = sb("span", [NSB, NG]), sb("spani", [NSB, NG], I32)
        slotf = sb("slotf", [NSB, NG])
        ftab, itab = sb("ftab_sb", [NSB, 2 * NG]), sb("itab_sb", [NSB, 2 * NG], I32)
        l2T = sb("l2T_sb", [MID, 4 * MID])
        l3 = sb("l3_sb", [MID, S + V])
        rowscale = sb("rowscale", [MID, 1])
        node_ps = [ctx.enter_context(nc.psum_tensor(f"node_ps{b}", [P, 512], F32)) for b in range(NBUF)]
        w3_ps = ctx.enter_context(nc.psum_tensor("w3_ps", [MID, 512], F32))

        weights_in = sem("weights_in")
        x_in = [sem(f"x_in{b}") for b in range(2)]
        dst_in, l_in, attrs_in, chain = sem("dst_in"), sem("l_in"), sem("attrs_in"), sem("chain")
        node_mm = sem("node_mm")
        part_done = sem("part_done")
        x1_done = sem("x1_done")
        x1_out = [sem(f"x1_out{b}") for b in range(2)]
        w3_mm, tab_done, tab_out, scale_set = sem("w3_mm"), sem("tab_done"), sem("tab_out"), sem("scale_set")
        block = ctx.enter_context(nc.Block())

        @block.sync
        def _(sp):
            def load(c, b):
                nodes = bass.ds(c * (CH * P), CH * P)
                sp.dma_start(vT[b][:], q["xT"][0:P, nodes]).then_inc(x_in[b], 16)
                sp.dma_start(sT[b][:], q["xT"][VS:D, nodes]).then_inc(x_in[b], 16)

            def store(c, b):
                sp.wait_ge(x1_done, (c + 1) * CH + NBUF)
                sp.dma_start(q["x1_rows"][:, bass.ds(c * CH, CH), :], x1[b][:]).then_inc(x1_out[b], 16)

            sp.dma_start(wv[:], q["wv_l1"]).then_inc(weights_in, 16)
            sp.dma_start(ws[:], q["ws_l1"]).then_inc(weights_in, 16)
            for b in range(2):
                load(b, b)
            with sp.Fori(0, NCH // 2 - 1) as i:
                for b in range(2):
                    sp.wait_ge(node_mm, (2 * i + b + 1) * CH)
                    load(2 * i + b + 2, b)
                    store(2 * i + b, b)
            for b in range(2):
                store(NCH - 2 + b, b)
            for b in range(2):
                sp.wait_ge(x1_out[b], (NCH // 2 + 1) * 16)

        @block.scalar
        def _(act):
            act.dma_start(keep["attrs"][:], q["attrs"]).then_inc(attrs_in, 16)
            act.dma_start(dst[:], q["dst_rows"]).then_inc(dst_in, 16)
            for to, of in ((l2T, "l2T"), (l3, "l3"), (keep["wv_sc"], "wv_sc"), (keep["ws_sc"], "ws_sc"),
                           (keep["iden"], "iden")):
                act.dma_start(to[:], q[of]).then_inc(l_in, 16)
            act.wait_ge(attrs_in, 16)
            with act.Fori(0, NCH // 2) as i:
                for u in range(2 * CH):
                    n = i * (2 * CH) + u
                    act.wait_ge(node_mm, n + 1)
                    act.wait_ge(x1_done, n + 1)
                    nc.scalar.activation(part[u % NBUF][:], node_ps[u % NBUF][:, 0:D], ACT.Copy,
                                         scale=keep["attrs"][:, bass.ds(n * 3, 1)]).then_inc(part_done, 1)
            act.wait_ge(l_in, 80)
            act.wait_ge(tab_done, 1)
            act.dma_start(q["ftab"], ftab[:]).then_inc(tab_out, 16)
            act.dma_start(q["itab"], itab[:]).then_inc(tab_out, 16)
            act.wait_ge(tab_out, 32)

        @block.tensor
        def _(pe):
            pe.wait_ge(weights_in, 32)
            with pe.Fori(0, NCH // 2) as i:
                for u in range(2 * CH):
                    b, t = u // CH, u % CH
                    n = i * (2 * CH) + u
                    if t == 0:
                        pe.wait_ge(x_in[b], i * 32 + 32)
                    pe.wait_ge(x1_done, n + 1)
                    ps = node_ps[u % NBUF][:, 0:2 * D].rearrange("p (k d) -> p k d", k=2)
                    nc.tensor.matmul(ps[:, :, 0:VS], vT[b][:, t * P:(t + 1) * P], wv[:], start=True, stop=False,
                                     skip_group_check=True)
                    nc.tensor.matmul(ps[:, :, VS:D], sT[b][:, t * P:(t + 1) * P], ws[:], start=False, stop=True,
                                     skip_group_check=True).then_inc(node_mm, 1)
            pe.wait_ge(l_in, 80)
            for k in range(2):
                nc.tensor.matmul(w3_ps[:, k * S:(k + 1) * S], l2T[:, k * MID:(k + 1) * MID], l3[:, 0:S],
                                 start=True, stop=True)
            for k in range(2):
                mm = nc.tensor.matmul(w3_ps[:, 2 * S + k * V:2 * S + (k + 1) * V],
                                      l2T[:, (2 + k) * MID:(3 + k) * MID], l3[:, S:], start=True, stop=True)
            mm.then_inc(w3_mm, 1)

        @block.gpsimd
        def _(pool):
            nc.gpsimd.memset(rowscale[0:S, :], 1.0).then_inc(scale_set, 1)
            pool.wait_ge(scale_set, 1)
            nc.gpsimd.memset(rowscale[S:MID, :], float(3.0 ** -0.5)).then_inc(scale_set, 1)
            pool.wait_ge(scale_set, 2)
            nc.gpsimd.iota(keep["iota32"][:], pattern=[[1, WIN]], base=0, channel_multiplier=0,
                           allow_small_or_imprecise_dtypes=True).then_inc(scale_set, 1)
            for blk in range(P // WIN):
                pool.wait_ge(scale_set, 3 + blk)
                nc.gpsimd.iota(keep["iota_row"][blk * WIN:(blk + 1) * WIN, :], pattern=[[1, 1]], base=0,
                               channel_multiplier=1, allow_small_or_imprecise_dtypes=True).then_inc(scale_set, 1)
            pool.wait_ge(scale_set, 3 + P // WIN)
            nc.gpsimd.memset(keep["agg"][:], 0.0)

        @block.vector
        def _(dve):
            links = [0]

            def link(ins):
                links[0] += 1
                ins.then_inc(chain, 1)
                dve.wait_ge(chain, links[0])

            nc.vector.sem_inc(x1_done, NBUF)
            for b in range(2):
                nc.vector.sem_inc(x1_out[b], 16)
            dve.wait_ge(attrs_in, 16)
            attr2 = keep["attrs"][:].rearrange("p (t c) -> p t c", c=3)
            scales = keep["scales"][:].rearrange("p (t c) -> p t c", c=4)
            nc.vector.tensor_scalar(scales[:, :, 0:2], attr2[:, :, 0:2], C_S, None, ALU.mult)
            nc.vector.scalar_tensor_tensor(scales[:, :, 2:4], attr2[:, :, 0:2], C_X / NEIGHBORS ** 0.5,
                                           attr2[:, :, 2:3].to_broadcast([P, NT, 2]), ALU.mult, ALU.mult)
            dve.wait_ge(dst_in, 16)
            nodes = dst[:].rearrange("p (s e) -> p s e", s=NSUB)
            for to, op in ((first, ALU.min), (last, ALU.max)):
                kinds = to[:].rearrange("p (s k) -> p s k", k=2)
                nc.vector.tensor_reduce(kinds[:, :, 0:1], nodes[:, :, 0:GT[0] * P], AX.X, op)
                link(nc.vector.tensor_reduce(kinds[:, :, 1:2], nodes[:, :, GT[0] * P:], AX.X, op))
            for to in (first, last):
                link(nc.vector.tensor_scalar(to[:], to[:], 0.0, float(N - 1), ALU.max, ALU.min))
            nc.vector.tensor_copy(firsti[:], first[:])
            link(nc.vector.tensor_tensor(span[:], last[:], first[:], ALU.subtract))
            link(nc.vector.tensor_copy(spani[:], span[:]))
            link(nc.vector.tensor_single_scalar(sloti[:], firsti[:], 5, ALU.arith_shift_right))
            nc.vector.tensor_single_scalar(itab[:, NG:], spani[:], 5, ALU.arith_shift_right)
            link(nc.vector.tensor_copy(slotf[:], sloti[:]))
            nc.vector.tensor_copy(ftab[:, 0:NG], first[:])
            nc.vector.tensor_scalar(ftab[:, NG:], slotf[:], float(WIN), None, ALU.mult)
            nc.vector.tensor_scalar(itab[:, 0:NG], slotf[:], float(MID), None, ALU.mult).then_inc(tab_done, 1)
            with dve.Fori(0, NCH // 2) as i:
                for u in range(2 * CH):
                    b, t = u // CH, u % CH
                    n = i * (2 * CH) + u
                    dve.wait_ge(part_done, n + 1)
                    if t == 0:
                        dve.wait_ge(x1_out[b], i * 16 + 16)
                    nc.vector.scalar_tensor_tensor(
                        x1[b][:, t, :], node_ps[u % NBUF][:, D:2 * D], keep["attrs"][:, bass.ds(n * 3 + 1, 1)],
                        part[u % NBUF][:], ALU.mult, ALU.add).then_inc(x1_done, 1)
            dve.wait_ge(w3_mm, 1)
            dve.wait_ge(scale_set, 2)
            nc.vector.tensor_scalar(keep["w3s"][:], w3_ps[:, 0:2 * S], rowscale[:], None, ALU.mult)
            nc.vector.tensor_copy(keep["w3v"][:], w3_ps[:, 2 * S:2 * S + 2 * V])


def edge_phase(nc, q, keep):
    with ExitStack() as ctx:
        sb = lambda name, shape, dt=F32: ctx.enter_context(nc.sbuf_tensor(name, shape, dt))
        ps = lambda name, cols: ctx.enter_context(nc.psum_tensor(name, [P, cols], F32))
        sem = lambda name: ctx.enter_context(nc.semaphore(name))
        agg = keep["agg"]
        w1 = sb("w1", [W_ROWS, H], BF16)
        w1_part = [sb(f"w1_part{k}", [W_ROWS, H], BF16) for k in range(3)]
        part_rows = sb("part_rows_sb", [W_ROWS, 3])
        raw = [sb(f"raw{b}", [P, RAW]) for b in range(2)]
        rest = sb("rest", [P, RAW])
        parts = [sb(f"parts{b}", [P, 3, RAW], BF16) for b in range(2)]
        w2 = sb("w2", [H, 2 * MID])
        rows_at = keep["iden"]
        src = [sb(f"src{b}", [P, ST], I32) for b in range(2)]
        dsti = [sb(f"dsti{b}", [P, ST], I32) for b in range(2)]
        ea = [sb(f"ea{b}", [P, ST, 4]) for b in range(2)]
        tab = [sb(f"tab{b}", [P, 2 * NG]) for b in range(2)]
        regs_row = [sb(f"regs_row{b}", [1, 2 * NG], I32) for b in range(2)]
        elen = [sb(f"elen{b}", [W_ROWS, NSUB, SUB * P], BF16) for b in range(2)]
        gat = sb("gat", [P, ST, D])
        hid = [sb(f"hid{k}", [H, GT[k] * P]) for k in range(2)]
        w1_raw, w1_rest = (hid[k][0:W_ROWS, 0:H] for k in range(2))
        feat = [sb(f"feat{k}", [P, GT[k], 2, D]) for k in range(2)]
        hot = [sb(f"hot{k}", [P, GT[k], WIN]) for k in range(2)]
        sel = [sb(f"sel{k}", [P, GT[k], 4, WIN]) for k in range(2)]
        dstf = sb("dstf", [P, ST])
        rel = [sb(f"rel{b}", [P, ST]) for b in range(2)]
        off = [sb(f"off{b}", [P, ST]) for b in range(2)]
        wrap, beyond = sb("wrap", [P, ST]), sb("beyond", [P, ST])
        row = [sb(f"row{b}", [P, ST]) for b in range(2)]
        m = sb("m", [P, NG])
        keep_lo = [sb(f"keep_lo{b}", [P, NG]) for b in range(2)]
        keep_hi = [sb(f"keep_hi{b}", [P, NG]) for b in range(2)]
        stage = [sb(f"stage{k}", [P, VS]) for k in range(2)]
        xrel, xoff, xrow, xa = sb("xrel", [P, GT[0]]), sb("xoff", [P, GT[0]]), sb("xrow", [P, GT[0]]), sb("xa", [P, GT[0]])
        xhot = sb("xhot", [P, GT[0], WIN])
        xsel = sb("xsel", [P, GT[0], 4, WIN])
        xstage = sb("xstage", [P, VS])
        vT, sT = sb("e_vT", [VS, P]), sb("e_sT", [S, P])
        res = sb("e_res", [P, D])

        hid_ps = [ps(f"hid_ps{k}", 512) for k in range(2)]
        wgt_ps = [ps("wgt_ps0", 1024), ps("wgt_ps1", 512)]
        win_ps = [ps(f"win_ps{k}", 512) for k in range(2)]
        xwin_ps = ps("xwin_ps", 512)

        const_in, w1_step = sem("const_in"), sem("w1_step")
        raw_in = [sem(f"raw_in{b}") for b in range(2)]
        high_done = sem("high_done")
        rest_done = sem("rest_done")
        middle_done = sem("middle_done")
        parts_done = sem("parts_done")
        parts_out = [sem(f"parts_out{b}") for b in range(2)]
        src_in = [sem(f"src_in{b}") for b in range(2)]
        edge_in = [sem(f"edge_in{b}") for b in range(2)]
        row_in = [sem(f"row_in{b}") for b in range(2)]
        len_in = [sem(f"len_in{b}") for b in range(2)]
        gat_in = [sem(f"gat_in{j}") for j in range(NG)]
        hid_mm = sem("hid_mm")
        silu_done = sem("silu_done")
        wgt_mm = sem("wgt_mm")
        feat_done = sem("feat_done")
        sel_done = sem("sel_done")
        win_mm = sem("win_mm")
        stage_done = sem("stage_done")
        swap_mm = sem("swap_mm")
        agg_done = sem("agg_done")
        slots_seen, counts_read = sem("slots_seen"), sem("counts_read")
        row_seen, half_done = sem("row_seen"), sem("half_done")
        hot_done, prep, rows_done = sem("hot_done"), sem("prep"), sem("rows_done")
        x_ready, x_win, x_stage, x_swap, x_chain = (sem(n) for n in ("x_ready", "x_win", "x_stage", "x_swap", "x_chain"))
        x_added = sem("x_added")
        self_mm = sem("self_mm")
        self_done = sem("self_done")
        node_in, node_out = sem("node_in"), sem("node_out")
        block = ctx.enter_context(nc.Block())

        def tile0(j):
            return (j // 2) * SUB + (j % 2) * GT[0]

        @block.sync
        def _(sp):
            def load_node(n):
                sp.dma_start(vT[:], q["xT"][0:VS, bass.ds(n * P, P)]).then_inc(node_in, 16)
                sp.dma_start(sT[:], q["xT"][VS:D, bass.ds(n * P, P)]).then_inc(node_in, 16)
                sp.dma_start(res[:], q["x"][bass.ds(n * P, P), :]).then_inc(node_in, 16)

            def store_node(n):
                sp.wait_ge(self_done, n + 2)
                sp.dma_start(q["res"][bass.ds(n * P, P), :], res[:]).then_inc(node_out, 16)
                sp.wait_ge(node_out, n * 16 + 16)

            def load_src(n, b):
                sp.dma_start(src[b][:], q["src_cols"][bass.ds(n, 1)].rearrange("a p t -> p (a t)")
                             ).then_inc(src_in[b], 16)

            def next_src(n, b):
                for j in range(NG):
                    sp.wait_ge(gat_in[j], n * (16 * GT[j % 2]) + 16 * GT[j % 2])
                load_src(n + 2, b)

            def load_raw(m, b):
                sp.dma_start(raw[b][:], q["elen"][bass.ds(m, 1)].rearrange("a p c -> p (a c)")).then_inc(raw_in[b], 16)

            def store_parts(m, b):
                sp.wait_ge(parts_done, m + 1)
                sp.dma_start(q["parts"][bass.ds(m, 1)].rearrange("a k (p c) -> p (a k) c", p=P),
                             parts[b][:]).then_inc(parts_out[b], 16)
                load_raw(m + 2, b)

            def load_parts(m, i, b):
                sp.wait_ge(parts_out[b], i * 16 + 32)
                row0 = 0
                for k, times in ((0, 3), (1, 2), (2, 1)):
                    for t in range(times):
                        sp.dma_start(elen[b][row0:row0 + NB].rearrange("r s e -> r (s e)"),
                                     q["parts"][bass.ds(m, 1), k, :].rearrange("a (r e) -> r (a e)", r=NB)
                                     ).then_inc(len_in[b], 16)
                        row0 += NB

            def load(n, b):
                row0 = bass.ds(n, 1)
                sp.dma_start(dsti[b][:], q["dst_cols"][row0].rearrange("a p t -> p (a t)")).then_inc(edge_in[b], 16)
                sp.dma_start(ea[b][:].rearrange("p t c -> p (t c)"),
                             q["ea"][row0].rearrange("a p t -> p (a t)")).then_inc(edge_in[b], 16)
                sp.dma_start(tab[b][:], q["ftab"][row0, :].to_broadcast([P, 2 * NG])).then_inc(edge_in[b], 16)
                sp.dma_start(regs_row[b][:], q["itab"][row0, :]).then_inc(row_in[b], 16)

            for b in range(2):
                load_src(b, b)
            for b in range(2):
                load_raw(b, b)
            sp.dma_start(w1_raw, q["w1"]).then_inc(const_in, 16)
            sp.dma_start(part_rows[:], q["part_rows"]).then_inc(const_in, 16)
            sp.dma_start(w2[:], q["w2"]).then_inc(const_in, 16)

            def next_load(n, i, b):
                sp.wait_ge(agg_done, (n + 1) * NG + 2)
                sp.wait_ge(counts_read, n + 1)
                load(n + 2, b)
                load_parts(n + 2, i + 1, b)

            for b in range(2):
                load(b, b)
            load_node(0)
            for m in range(AHEAD):
                store_parts(m, m % 2)
                if m:
                    load_parts(m - 1, 0, m - 1)
            with sp.Fori(0, NT // 2 - 1) as i:
                for b in range(2):
                    next_src(2 * i + b, b)
                    store_parts(2 * i + b + AHEAD, (b + AHEAD) % 2)
                    store_node(2 * i + b)
                    load_node(2 * i + b + 1)
                    next_load(2 * i + b, i, b)
            for b in range(2):
                next_src(NT - 2 + b, b)
                store_parts(NT - 2 + b + AHEAD, (b + AHEAD) % 2)
                store_node(NT - 2 + b)
                if b == 0:
                    load_node(NT - 1)
                next_load(NT - 2 + b, NT // 2 - 1, b)
            with sp.Fori(NT // 2, (NSB - 3) // 2) as i:
                for b in range(2):
                    next_src(2 * i + b, b)
                    store_parts(2 * i + b + AHEAD, (b + AHEAD) % 2)
                    next_load(2 * i + b, i, b)
            next_src(NSB - 3, 0)
            store_parts(NSB - 3 + AHEAD, (NSB - 3 + AHEAD) % 2)
            next_load(NSB - 3, (NSB - 3) // 2, 0)
            for b in range(2):
                stores = len(range(b, NSB - 2 + AHEAD, 2))
                sp.wait_ge(parts_out[b], 16 * stores + 16)
                sp.wait_ge(raw_in[b], 16 * stores + 16)

        def superblocks(eng, body):
            for i0, i1, node in ((0, NT // 2, True), (NT // 2, NSB // 2, False)):
                with eng.Fori(i0, i1) as i:
                    for b in range(2):
                        body(2 * i + b, i, b, node, False)
            body(NSB - 1, NSB // 2, 0, False, True)

        @block.gpsimd
        def _(pool):
            def body(n, i, b, node, last):
                pool.wait_ge(src_in[b], i * 16 + 16)
                for j in range(NG):
                    pool.wait_ge(feat_done, n * NG + j + 1)
                    nc.gpsimd.sem_inc(slots_seen, 1)
                    for t in range(tile0(j), tile0(j) + GT[j % 2]):
                        nc.gpsimd.indirect_dma_start(
                            out=gat[:, t, :], out_offset=None, in_=q["x1"],
                            in_offset=bass.IndirectOffsetOnAxis(ap=src[b][:, t:t + 1], axis=0)
                        ).then_inc(gat_in[j], 16)
            superblocks(pool, body)

        @block.scalar
        def _(act):
            nc.scalar.sem_inc(silu_done, 2)

            def silu(g, k):
                act.wait_ge(hid_mm, g + 1)
                act.wait_ge(wgt_mm, g + 1)
                nc.scalar.activation(hid[k][:], hid_ps[k][0:H, 0:GT[k] * P], ACT.Silu).then_inc(silu_done, 1)

            def high_part(m, i, b):
                act.wait_ge(raw_in[b], i * 16 + 16)
                act.wait_ge(parts_out[b], i * 16 + 16)
                nc.scalar.activation(parts[b][:, 0, :], raw[b][:], ACT.Copy).then_inc(high_done, 1)

            def middle_part(m, i, b):
                act.wait_ge(rest_done, m + 1)
                nc.scalar.activation(parts[b][:, 1, :], rest[:], ACT.Copy).then_inc(middle_done, 1)

            def body(n, i, b, node, last):
                for j in range(NG):
                    g, k = n * NG + j, j % 2
                    act.wait_ge(win_mm, g + 3)
                    act.wait_ge(swap_mm, g + 1)
                    nc.scalar.activation(stage[k][:], win_ps[k][:, 0:VS], ACT.Copy).then_inc(stage_done, 1)
                    if not (last and j + 3 >= NG):
                        silu(g + 3, (j + 3) % 2)
                    if not last and j in (1, 4):
                        (high_part if j == 1 else middle_part)(n + AHEAD, i + (b + AHEAD) // 2, (b + AHEAD) % 2)
            for m in range(AHEAD):
                high_part(m, m // 2, m % 2)
                middle_part(m, m // 2, m % 2)
            for g in range(3):
                silu(g, g % 2)
            superblocks(act, body)

        @block.tensor
        def _(pe):
            nc.tensor.sem_inc(wgt_mm, 2)
            nc.tensor.sem_inc(win_mm, 2)
            nc.tensor.sem_inc(swap_mm, 2)
            extra_regs = [pe.alloc_register(f"pe_extra{j}") for j in range(NG)]
            count = pe.alloc_register("pe_count")
            pe.reg_mov(count, 0)
            pe.wait_ge(const_in, 16 * 3)
            pe.wait_ge(w1_step, 7)

            def hidden(g, j, b, i):
                k = j % 2
                if j == 0:
                    pe.wait_ge(len_in[b], i * 96 + 96)
                pe.wait_ge(silu_done, g + 1)
                c0 = k * GT[0] * P
                nc.tensor.matmul(hid_ps[k][0:H, 0:GT[k] * P], w1[:], elen[b][:, j // 2, c0:c0 + GT[k] * P],
                                 start=True, stop=True).then_inc(hid_mm, 1)

            def weights(g, k):
                pe.wait_ge(silu_done, g + 3)
                pe.wait_ge(feat_done, g + NG - 1)
                for t in range(GT[k]):
                    mm = nc.tensor.matmul(wgt_ps[k][:, t * 256:t * 256 + 2 * MID], hid[k][:, t * P:(t + 1) * P],
                                          w2[:], start=True, stop=True)
                mm.then_inc(wgt_mm, 1)

            def window(to, one_hot, k):
                for t in range(GT[k]):
                    for c in range(4):
                        mm = nc.tensor.matmul(to[c * WIN:(c + 1) * WIN, 0:D], one_hot[:, t, c, :],
                                              feat[k][:, t, min(c, 1), :], start=t == 0, stop=t == GT[k] - 1,
                                              tile_position=(0, c * WIN))
                return mm

            def swapped(to, of):
                for c in range(3):
                    columns = of[:, c * V:(c + 1) * V]
                    there = (c + 1) * WIN
                    nc.tensor.matmul(to[there:there + WIN, D:D + V], rows_at[:, 0:WIN], columns, start=True, stop=True,
                                     tile_position=(0, there))
                    mm = nc.tensor.matmul(to[0:WIN, D:D + V], rows_at[:, there:there + WIN], columns, start=c == 0,
                                          stop=c == 2, tile_position=(0, 0))
                return mm

            def window_of(g, k):
                pe.wait_ge(feat_done, g + NG + 1)
                pe.wait_ge(sel_done, g + 1)
                pe.wait_ge(agg_done, g + 1)
                window(win_ps[k], sel[k], k).then_inc(win_mm, 1)

            def more_windows(k, extra):
                with pe.If(extra > 0):
                    with pe.Fori(0, extra) as _w:
                        pe.reg_add(count, count, 1)
                        pe.wait_ge(x_ready, pe.snap(count))
                        window(xwin_ps, xsel, k).then_inc(x_win, 1)
                        pe.wait_ge(x_stage, pe.snap(count))
                        swapped(xwin_ps, xstage).then_inc(x_swap, 1)
                        pe.wait_ge(x_added, pe.snap(count))

            hidden(0, 0, 0, 0)
            hidden(1, 1, 0, 0)
            weights(0, 0)
            hidden(2, 2, 0, 0)
            weights(1, 1)
            window_of(0, 0)

            def body(n, i, b, node, last):
                pe.wait_ge(row_in[b], i * 16 + 16)
                nc.tensor.sem_inc(row_seen, 1)
                pe.reg_load(extra_regs, regs_row[b][0:1, NG:])
                nc.tensor.sem_inc(counts_read, 1)
                for j in range(NG):
                    g, k = n * NG + j, j % 2
                    more_windows(k, pe.snap(extra_regs[j], min_val=0, max_val=SLOTS))
                    if node and j == NG // 2:
                        pe.wait_ge(node_in, n * 48 + 48)
                        pe.wait_ge(self_done, n + 1)
                        to = xwin_ps[:, 0:2 * D].rearrange("p (k d) -> p k d", k=2)
                        nc.tensor.matmul(to[:, :, 0:VS], vT[:], keep["wv_sc"][:], start=True, stop=False,
                                         skip_group_check=True)
                        nc.tensor.matmul(to[:, :, VS:D], sT[:], keep["ws_sc"][:], start=False, stop=True,
                                         skip_group_check=True).then_inc(self_mm, 1)
                    if not (last and j + 2 >= NG):
                        weights(g + 2, k)
                    if not (last and j + 3 >= NG):
                        over = j + 3 >= NG
                        hidden(g + 3, (j + 3) % NG, (b + 1) % 2 if over else b, i + b if over else i)
                    pe.wait_ge(stage_done, g + 1)
                    swapped(win_ps[k], stage[k]).then_inc(swap_mm, 1)
                    if not (last and j + 1 >= NG):
                        window_of(g + 1, 1 - k)
            superblocks(pe, body)

        @block.vector
        def _(dve):
            nc.vector.sem_inc(feat_done, NG)
            nc.vector.sem_inc(agg_done, 2)
            nc.vector.sem_inc(self_done, 1)
            slot_regs = [dve.alloc_register(f"dve_slot{j}") for j in range(NG)]
            extra_regs = [dve.alloc_register(f"dve_extra{j}") for j in range(NG)]
            count = dve.alloc_register("dve_count")
            dve.reg_mov(count, 0)
            PREP = 4

            def kinds(ap):
                v = ap.rearrange("p (s t) -> p s t", t=SUB)
                return v[:, :, 0:GT[0]], v[:, :, GT[0]:]

            def split_w1():
                step = [0]

                def stepped(ins):
                    step[0] += 1
                    ins.then_inc(w1_step, 1)
                    dve.wait_ge(w1_step, step[0])

                dve.wait_ge(const_in, 48)
                stepped(nc.vector.tensor_copy(w1_part[0][:], w1_raw))
                stepped(nc.vector.tensor_tensor(w1_rest, w1_raw, w1_part[0][:], ALU.subtract))
                stepped(nc.vector.tensor_copy(w1_part[1][:], w1_rest))
                stepped(nc.vector.tensor_tensor(w1_part[2][:], w1_rest, w1_part[1][:], ALU.subtract))
                stepped(nc.vector.tensor_scalar(w1[:], w1_part[0][:], part_rows[:, 0:1], None, ALU.mult))
                for k in (1, 2):
                    stepped(nc.vector.scalar_tensor_tensor(w1[:], w1_part[k][:], part_rows[:, k:k + 1], w1[:],
                                                           ALU.mult, ALU.add))

            def split_rest(m, b):
                if not (isinstance(m, int) and m == 0):
                    dve.wait_ge(parts_done, m)
                dve.wait_ge(high_done, m + 1)
                nc.vector.tensor_tensor(rest[:], raw[b][:], parts[b][:, 0, :], ALU.subtract).then_inc(rest_done, 1)

            def low_part(m, b):
                dve.wait_ge(middle_done, m + 1)
                nc.vector.tensor_tensor(parts[b][:, 2, :], rest[:], parts[b][:, 1, :], ALU.subtract
                                        ).then_inc(parts_done, 1)

            def rows(n, i, b, step):
                if step == 0:
                    dve.wait_ge(edge_in[b], i * 48 + 48)
                    nc.vector.tensor_copy(dstf[:], dsti[b][:])
                    nc.vector.tensor_tensor(m[:], tab[b][:, 0:NG], tab[b][:, NG:], ALU.subtract).then_inc(prep, 1)
                    return
                dve.wait_ge(prep, n * PREP + step)
                if step == 1:
                    first = tab[b][:, 0:NG].rearrange("p (s k) -> p s k", k=2)
                    slot0 = tab[b][:, NG:].rearrange("p (s k) -> p s k", k=2)
                    for k in range(2):
                        shape = [P, NSUB, GT[k]]
                        nc.vector.tensor_tensor(kinds(rel[b][:])[k], kinds(dstf[:])[k],
                                                first[:, :, k:k + 1].to_broadcast(shape), ALU.subtract)
                        nc.vector.tensor_tensor(kinds(off[b][:])[k], kinds(dstf[:])[k],
                                                slot0[:, :, k:k + 1].to_broadcast(shape), ALU.subtract)
                    nc.vector.tensor_scalar(keep_lo[b][:], m[:], keep["iota_row"][:], None, ALU.is_le)
                    nc.vector.tensor_scalar(keep_hi[b][:], m[:], keep["iota_row"][:], None, ALU.is_gt).then_inc(prep, 1)
                elif step == 2:
                    nc.vector.tensor_scalar(wrap[:], off[b][:], float(WIN), -float(WIN), ALU.is_ge, ALU.mult)
                    nc.vector.tensor_scalar(beyond[:], rel[b][:], float(WIN), 1000.0, ALU.is_ge, ALU.mult).then_inc(prep, 1)
                elif step == 3:
                    nc.vector.tensor_tensor(wrap[:], wrap[:], beyond[:], ALU.add).then_inc(prep, 1)
                else:
                    nc.vector.tensor_tensor(row[b][:], off[b][:], wrap[:], ALU.add).then_inc(rows_done, 1)

            def one_hot(to, rows_of, k):
                shape = [P, GT[k], WIN]
                return nc.vector.tensor_tensor(to[:, 0:GT[k], :], keep["iota32"][:, None, :].to_broadcast(shape),
                                               rows_of[:, :, None].to_broadcast(shape), ALU.is_equal)

            def scaled(to, hots, b, t0, k):
                shape = [P, GT[k], 4, WIN]
                return nc.vector.tensor_tensor(to[:, 0:GT[k]], hots[:, 0:GT[k], None, :].to_broadcast(shape),
                                               ea[b][:, t0:t0 + GT[k], :, None].to_broadcast(shape), ALU.mult)

            def block_of(g, n, i, b, j):
                k, t0 = j % 2, tile0(j)
                if j == 0:
                    dve.wait_ge(rows_done, n + 1)
                dve.wait_ge(win_mm, g + 1)
                one_hot(hot[k], row[b][:, t0:t0 + GT[k]], k).then_inc(hot_done, 1)
                dve.wait_ge(wgt_mm, g + 3)
                dve.wait_ge(gat_in[j], n * (16 * GT[k]) + 16 * GT[k])
                T = GT[k]
                w = wgt_ps[k][:].rearrange("p (t c) -> p t c", c=256)[:, 0:T, :]
                rows_g = gat[:, t0:t0 + T, :]
                nc.vector.tensor_tensor(
                    feat[k][:, :, :, VS:D], w[:, :, 0:2 * S].rearrange("p t (h s) -> p t h s", h=2),
                    rows_g[:, :, None, VS:D].to_broadcast([P, T, 2, S]), ALU.mult)
                for h in range(2):
                    f = nc.vector.tensor_tensor(
                        feat[k][:, :, h, 0:VS].rearrange("p t (c u) -> p t c u", c=3),
                        w[:, :, None, 2 * S + h * V:2 * S + (h + 1) * V].to_broadcast([P, T, 3, V]),
                        rows_g[:, :, 0:VS].rearrange("p t (c u) -> p t c u", c=3), ALU.mult)
                f.then_inc(feat_done, 1)
                dve.wait_ge(hot_done, g + 1)
                scaled(sel[k], hot[k], b, t0, k).then_inc(sel_done, 1)

            def add_window(win, col, b, j):
                for half, mask in ((0, keep_lo), (1, keep_hi)):
                    to = agg[:, bass.ds(col + half * MID, MID)]
                    last = nc.vector.scalar_tensor_tensor(to, win[:, VS:D + V], mask[b][:, j:j + 1], to,
                                                          ALU.mult, ALU.add)
                return last

            def more_windows(b, j, extra):
                k, t0 = j % 2, tile0(j)
                T = GT[k]
                tiles = slice(t0, t0 + T)
                with dve.If(extra > 0):
                    nc.vector.tensor_copy(xrel[:, 0:T], rel[b][:, tiles])
                    nc.vector.tensor_copy(xoff[:, 0:T], off[b][:, tiles])
                    nc.vector.drain()
                    with dve.Fori(0, extra) as _w:
                        dve.reg_add(count, count, 1)
                        dve.reg_add(slot_regs[j], slot_regs[j], MID)
                        for a in (xrel, xoff):
                            nc.vector.tensor_scalar(a[:, 0:T], a[:, 0:T], -float(WIN), None, ALU.add)
                        nc.vector.drain()
                        for of, lim, op, val in ((xoff, float(WIN), ALU.is_ge, -float(WIN)),
                                                 (xrel, float(WIN), ALU.is_ge, 1000.0),
                                                 (xrel, 0.0, ALU.is_lt, 1000.0)):
                            nc.vector.tensor_scalar(xa[:, 0:T], of[:, 0:T], lim, val, op, ALU.mult)
                            nc.vector.drain()
                            nc.vector.tensor_tensor(xrow[:, 0:T], xoff[:, 0:T] if of is xoff else xrow[:, 0:T],
                                                    xa[:, 0:T], ALU.add)
                            nc.vector.drain()
                        one_hot(xhot, xrow[:, 0:T], k)
                        nc.vector.drain()
                        scaled(xsel, xhot, b, t0, k).then_inc(x_ready, 1)
                        dve.wait_ge(x_win, dve.snap(count))
                        nc.vector.tensor_copy(xstage[:], xwin_ps[:, 0:VS]).then_inc(x_stage, 1)
                        dve.wait_ge(x_swap, dve.snap(count))
                        add_window(xwin_ps, dve.snap(slot_regs[j], min_val=0, max_val=(SLOTS - 2) * MID), b, j).then_inc(x_added, 1)
                        nc.vector.drain()

            def self_part(n, i, b, h):
                if h:
                    dve.wait_ge(half_done, n + 1)
                else:
                    dve.wait_ge(node_in, n * 48 + 48)
                    dve.wait_ge(self_mm, n + 1)
                nc.vector.scalar_tensor_tensor(
                    res[:], xwin_ps[:, h * D:(h + 1) * D], keep["scales"][:, bass.ds(n * 4 + h, 1)],
                    res[:], ALU.mult, ALU.add).then_inc(self_done if h else half_done, 1)

            def body(n, i, b, node, last):
                dve.wait_ge(row_in[b], i * 16 + 16)
                nc.vector.sem_inc(row_seen, 1)
                dve.reg_load(slot_regs + extra_regs, regs_row[b][0:1, :])
                for j in range(NG):
                    g = n * NG + j
                    col = dve.snap(slot_regs[j], min_val=0, max_val=(SLOTS - 2) * MID)
                    more_windows(b, j, dve.snap(extra_regs[j], min_val=0, max_val=SLOTS))
                    if not last and 3 <= j < 8:
                        rows(n + 1, i + b, (b + 1) % 2, j - 3)
                    if not last and j == 2:
                        split_rest(n + AHEAD, (b + AHEAD) % 2)
                    if not last and j == 6:
                        low_part(n + AHEAD, (b + AHEAD) % 2)
                    if not (last and j + 2 >= NG):
                        if j + 2 < NG:
                            block_of(g + 2, n, i, b, j + 2)
                        else:
                            block_of(g + 2, n + 1, i + b, (b + 1) % 2, j + 2 - NG)
                    if node and j == NG // 2:
                        self_part(n, i, b, 0)
                    dve.wait_ge(swap_mm, g + 3)
                    dve.wait_ge(agg_done, g + 2)
                    add_window(win_ps[j % 2], col, b, j).then_inc(agg_done, 1)
                    if node and j == NG // 2:
                        self_part(n, i, b, 1)

            for b in range(2):
                nc.vector.sem_inc(parts_out[b], 16)
            for m_ in range(AHEAD):
                split_rest(m_, m_ % 2)
                low_part(m_, m_ % 2)
                if m_ == 0:
                    split_w1()
            for step in range(PREP + 1):
                rows(0, 0, 0, step)
            block_of(0, 0, 0, 0, 0)
            block_of(1, 0, 0, 0, 1)
            superblocks(dve, body)


def node_phase(nc, q, keep):
    with ExitStack() as ctx:
        sb = lambda name, shape, dt=F32: ctx.enter_context(nc.sbuf_tensor(name, shape, dt))
        psum = lambda name: ctx.enter_context(nc.psum_tensor(name, [P, 512], F32))
        sem = lambda name: ctx.enter_context(nc.semaphore(name))
        agg = keep["agg"]
        W4 = P // WIN
        res = [sb(f"res{b}", [P, CH, D]) for b in range(2)]
        total = [sb(f"total{b}", [P, CH, D]) for b in range(2)]
        normed = [sb(f"normed{b}", [P, CH, D]) for b in range(2)]
        packed = [sb(f"packed{b}", [P, W4 * MID]) for b in range(2)]
        aggT = [sb(f"aggT{b}", [MID, 4, P]) for b in range(2)]
        stats = [sb(f"stats{b}", [P, 6]) for b in range(CH)]
        moments = [sb(f"moments{b}", [P, CH, 2]) for b in range(2)]
        rstd = [sb(f"rstd{b}", [P, CH]) for b in range(2)]
        epst = sb("epst", [P, 1])
        turn_ps = [psum(f"turn_ps{b}") for b in range(2)]
        out_ps = [psum(f"out_ps{b}") for b in range(2)]

        res_in = [sem(f"res_in{b}") for b in range(2)]
        packed_done = sem("packed_done")
        turn_mm = sem("turn_mm")
        turned = sem("turned")
        out_mm = sem("out_mm")
        half_sum = sem("half_sum")
        out_used = sem("out_used")
        stats_done, stats_seen = sem("stats_done"), sem("stats_seen")
        moments_done, rstd_done = sem("moments_done"), sem("rstd_done")
        eps_set, std_done = sem("eps_set"), sem("std_done")
        norm_done = sem("norm_done")
        stored = [sem(f"stored{b}") for b in range(2)]
        block = ctx.enter_context(nc.Block())
        TILES_2 = 2 * CH

        def tiles(eng, body):
            for u in range(TILES_2):
                body(u, u, 0, True, False)
            with eng.Fori(1, NCH // 2 - 1) as i:
                for u in range(TILES_2):
                    body(i * TILES_2 + u, u, i, False, False)
            for u in range(TILES_2):
                body(NT - TILES_2 + u, u, NCH // 2 - 1, False, True)

        @block.sync
        def _(sp):
            def load(c, b):
                sp.dma_start(res[b][:], q["res_rows"][:, bass.ds(c * CH, CH), :]).then_inc(res_in[b], 16)

            def store(c, b):
                sp.wait_ge(norm_done, (c + 1) * CH)
                sp.dma_start(q["out_rows"][:, bass.ds(c * CH, CH), :], normed[b][:]).then_inc(stored[b], 16)

            for b in range(2):
                load(b, b)
            with sp.Fori(0, NCH // 2 - 1) as i:
                for b in range(2):
                    c = 2 * i + b
                    sp.wait_ge(out_used, (c + 1) * CH + 2)
                    load(c + 2, b)
                    store(c, b)
            for b in range(2):
                store(NCH - 2 + b, b)
            for b in range(2):
                sp.wait_ge(stored[b], (NCH // 2 + 1) * 16)

        @block.tensor
        def _(pe):
            nc.tensor.sem_inc(out_mm, 2)

            def turn(n, u):
                pe.wait_ge(packed_done, n + 1)
                for w in range(W4):
                    mm = nc.tensor.transpose(turn_ps[u % 2][0:MID, w * P:(w + 1) * P],
                                             packed[u % 2][:, w * MID:(w + 1) * MID], keep["iden"][:])
                mm.then_inc(turn_mm, 1)

            def body(n, u, i, first, last):
                if not (last and u == TILES_2 - 1):
                    turn(n + 1, u + 1)
                pe.wait_ge(turned, n + 1)
                pe.wait_ge(out_used, n + 1)
                po = out_ps[u % 2][:, 0:2 * D].rearrange("p (k d) -> p k d", k=2)
                nc.tensor.matmul(po[:, :, VS:D], aggT[u % 2][:, 0, :], keep["w3s"][:], start=True, stop=True,
                                 skip_group_check=True)
                for v in range(3):
                    mm = nc.tensor.matmul(po[:, :, v * V:(v + 1) * V], aggT[u % 2][:, 1 + v, :], keep["w3v"][:],
                                          start=False, stop=True, skip_group_check=True)
                mm.then_inc(out_mm, 1)
            turn(0, 0)
            tiles(pe, body)

        @block.scalar
        def _(act):
            def pack(n, u):
                nc.scalar.activation(packed[u % 2][:], agg[:, bass.ds(n * (W4 * MID), W4 * MID)], ACT.Copy
                                     ).then_inc(packed_done, 1)

            def deviations(c, b):
                act.wait_ge(moments_done, c + 1)
                nc.scalar.activation(rstd[b][:], moments[b][:, :, 1], ACT.Sqrt, bias=epst[:]).then_inc(std_done, 1)

            def body(n, u, i, first, last):
                act.wait_ge(turn_mm, n + 1)
                act.wait_ge(out_mm, n + 1)
                nc.scalar.activation(aggT[u % 2][:].rearrange("m q (w r) -> m w q r", w=W4),
                                     turn_ps[u % 2][0:MID, :].rearrange("m (w q r) -> m w q r", w=W4, q=4),
                                     ACT.Copy).then_inc(turned, 1)
                if not (last and u >= TILES_2 - 2):
                    pack(n + 2, u)
                b = u // CH
                if u % CH == 3 and not (first and b == 0):
                    deviations(2 * i + b - 1, 1 - b)
            act.wait_ge(eps_set, 1)
            nc.scalar.activation(rstd[0][:, 0:1], epst[:], ACT.Sqrt).then_inc(std_done, 1)
            for n in range(2):
                pack(n, n)
            tiles(act, body)
            deviations(NCH - 1, 1)

        @block.vector
        def _(dve):
            nc.vector.sem_inc(out_used, 2)
            nc.vector.memset(epst[:], EPS).then_inc(eps_set, 1)
            for b in range(2):
                nc.vector.sem_inc(stored[b], 16)

            def normalize(c, b, i, tiles_of):
                for t in tiles_of:
                    if t == 0:
                        dve.wait_ge(std_done, c + 2)
                        nc.vector.reciprocal(rstd[b][:], rstd[b][:]).then_inc(rstd_done, 1)
                        dve.wait_ge(rstd_done, c + 1)
                        dve.wait_ge(stored[b], i * 16 + 16)
                    nc.vector.tensor_scalar(normed[b][:, t, :], total[b][:, t, :], moments[b][:, t, 0:1],
                                            rstd[b][:, t:t + 1], ALU.subtract, ALU.mult).then_inc(norm_done, 1)

            def statistics(n, c, b, t):
                dve.wait_ge(out_used, n + 3)
                nc.vector.bn_stats(stats[t][:], total[b][:, t, :]).then_inc(stats_done, 1)
                if t == CH - 1:
                    dve.wait_ge(stats_done, n + 1)
                    nc.vector.sem_inc(stats_seen, 1)
                    for k in range(CH):
                        last_aggr = nc.vector.bn_aggr(moments[b][:, k, :], stats[k][:])
                    last_aggr.then_inc(moments_done, 1)

            def body(n, u, i, first, last):
                b, t = u // CH, u % CH
                c = 2 * i + b
                earlier = not (first and b == 0)
                if t == 0:
                    dve.wait_ge(res_in[b], i * 16 + 16)
                dve.wait_ge(out_mm, n + 3)
                for h in range(2):
                    if h:
                        dve.wait_ge(half_sum, n + 1)
                    nc.vector.scalar_tensor_tensor(
                        total[b][:, t, :], out_ps[u % 2][:, h * D:(h + 1) * D],
                        keep["scales"][:, bass.ds(n * 4 + 2 + h, 1)], (total if h else res)[b][:, t, :],
                        ALU.mult, ALU.add).then_inc(out_used if h else half_sum, 1)
                    if h == 0 and t > 0:
                        statistics(n - 1, c, b, t - 1)
                    elif h == 0 and earlier:
                        statistics(n - 1, c - 1, 1 - b, CH - 1)
                    if 0 <= 2 * t + h - 6 < CH and earlier:
                        normalize(c - 1, 1 - b, i - (1 - b), (2 * t + h - 6,))

            tiles(dve, body)
            statistics(NT - 1, NCH - 1, 1, CH - 1)
            normalize(NCH - 1, 1, NCH // 2 - 1, range(CH))


def build(nc, a, out):
    q = dict(a)
    x1 = nc.dram_tensor("x1", [NP, D], F32, kind="Internal").ap()
    q["x1"] = x1
    q["x1_rows"] = x1.rearrange("(t p) d -> p t d", p=P)
    q["res"] = nc.dram_tensor("res", [NP, D], F32, kind="Internal").ap()
    q["res_rows"] = q["res"].rearrange("(t p) d -> p t d", p=P)
    q["parts"] = nc.dram_tensor("parts", [NSB + AHEAD, 3, NB * ST * P], BF16, kind="Internal").ap()
    q["out_rows"] = out.rearrange("(t p) d -> p t d", p=P)
    q["ftab"] = nc.dram_tensor("ftab", [NSB, 2 * NG], F32, kind="Internal").ap()
    q["itab"] = nc.dram_tensor("itab", [NSB, 2 * NG], I32, kind="Internal").ap()
    with ExitStack() as ctx:
        sb = lambda name, shape: ctx.enter_context(nc.sbuf_tensor(name, shape, F32))
        keep = {
            "agg": sb("agg", [P, SLOTS * MID]),
            "iota32": sb("iota32", [P, WIN]), "iota_row": sb("iota_row", [P, 1]),
            "attrs": sb("attrs_sb", [P, NT * 3]), "scales": sb("scales", [P, NT * 4]),
            "wv_sc": sb("wv_sc_sb", [VS, 2 * VS]), "ws_sc": sb("ws_sc_sb", [S, 2 * S]), "iden": sb("iden_sb", [P, P]),
            "w3s": sb("w3s", [MID, 2 * S]), "w3v": sb("w3v", [MID, 2 * V]),
        }
        prep_phase(nc, q, keep)
        edge_phase(nc, q, keep)
        node_phase(nc, q, keep)


def kernel(**inputs):
    import numpy as np
    import concourse.bacc as bacc
    from concourse.bass_utils import run_bass_kernel_spmd as run

    a = {k: np.asarray(v) for k, v in inputs.items()}
    w = {k[len("L0_gnn_"):]: v for k, v in a.items() if k.startswith("L0_gnn_")}

    def columns(x):
        v = x[:, S:].reshape(-1, V, 3).transpose(0, 2, 1).reshape(-1, VS)
        return np.concatenate([v, x[:, :S]], axis=1)

    def padded(x):
        out = np.zeros((NP,) + x.shape[1:], x.dtype)
        out[:N] = x
        return out

    def diagonal(kind):
        out = np.zeros((VS, 2, VS), np.float32)
        for h, name in enumerate("ac"):
            for c in range(3):
                out[c * V:(c + 1) * V, h, c * V:(c + 1) * V] = w[f"Wv_{kind}_{name}"]
        return out.reshape(VS, 2 * VS), np.concatenate([w[f"Ws_{kind}_{name}"] for name in "ac"], axis=1)

    xp = padded(columns(a["x"]))
    attrs = np.stack([padded(a[k][:, 0]) for k in ("node_vec1", "node_vec1_n2", "node_vec1_n3")], axis=1)
    l1, sc = diagonal("l1"), diagonal("sc")
    arrays = {
        "x": xp, "xT": xp.T, "attrs": attrs.reshape(NT, P, 3).transpose(1, 0, 2).reshape(P, NT * 3),
        "src_cols": a["src"].reshape(NSB, ST, P).transpose(0, 2, 1),
        "dst_cols": a["dst"].reshape(NSB, ST, P).transpose(0, 2, 1),
        "dst_rows": a["dst"].reshape(NSB, ST * P),
        "ea": a["edge_attr_4"].reshape(NSB, ST, P, 4).transpose(0, 2, 1, 3).reshape(NSB, P, ST * 4),
        "elen": a["edge_attr_10"].reshape(NSB, NSUB, SUB * P, NB).transpose(0, 3, 1, 2).reshape(NSB, P, RAW),
        "wv_l1": np.pad(l1[0], ((0, P - VS), (0, 0))), "ws_l1": l1[1], "wv_sc": sc[0], "ws_sc": sc[1],
        "w1": np.tile(w["W_fc1"], (6, 1)),
        "part_rows": np.repeat(np.eye(3, dtype=np.float32)[[0, 1, 2, 0, 1, 0]], NB, axis=0), "w2": w["W_fc2"],
        "l2T": np.stack([w[k].T for k in ("Ws_l2_a", "Ws_l2_c", "Wv_l2_a", "Wv_l2_c")], axis=1).reshape(MID, 4 * MID),
        "l3": np.concatenate([w["Ws_l3"], w["Wv_l3"]], axis=1),
        "iden": np.eye(P, dtype=np.float32),
    }
    arrays["elen"] = np.pad(arrays["elen"], ((0, AHEAD), (0, 0), (0, 0)))
    nc = bacc.Bacc("TRN2", target_bir_lowering=False, num_devices=1)
    aps, feed = {}, {}
    for name, x in arrays.items():
        feed[f"in_{name}"] = np.ascontiguousarray(x)
        aps[name] = nc.dram_tensor(f"in_{name}", x.shape, mybir.dt.from_np(x.dtype), kind="ExternalInput").ap()
    out = nc.dram_tensor("out_0", (NP, D), F32, kind="ExternalOutput").ap()
    build(nc, aps, out)
    got = run(nc, [feed], core_ids=[0]).results[0]["out_0"][:N]
    return np.concatenate([got[:, VS:], got[:, :VS].reshape(N, 3, V).transpose(0, 2, 1).reshape(N, VS)], axis=1)
```
